# Optimizing a Trainium2 kernel written in Bass

```python
import numpy as np
import jax
import jax.numpy as jnp

def _softmax(x, axis=-1):
    return jax.nn.softmax(x, axis=axis)

def _gelu(x):
    return jax.nn.gelu(x, approximate=True)

def _silu(x):
    return jax.nn.silu(x)

def _sigmoid(x):
    return jax.nn.sigmoid(x)

def _layernorm(x, axis=-1, eps=1e-05):
    m = jnp.mean(x, axis=axis, keepdims=True)
    v = jnp.var(x, axis=axis, keepdims=True)
    return (x - m) / jnp.sqrt(v + eps)

def _scatter_add(tgt, idx, src, axis=0):
    return tgt.at[idx].add(src)

def _segment_sum(src, seg, n):
    return jax.ops.segment_sum(src, seg, n)
kernel_name = 'mk_macaron_d1_jaxref_r8_78276a'

def setup_inputs(seed: int=0):
    np.random.seed(seed)
    _w = jnp.asarray

    def _L0_attn_setup():
        import jax, jax.numpy as jnp
        import numpy as np
        B, S, D = (4, 512, 128)
        H = 8
        DK = D // H
        DV = D // H
        KLEPE = 5
        ROPE_BASE = 10000.0

        def rotate_half(x):
            x1, x2 = jnp.split(x, 2, axis=-1)
            return jnp.concatenate([-x2, x1], axis=-1)

        def rope_sin_cos(seq_len, dim):
            inv_freq = 1.0 / ROPE_BASE ** (jnp.arange(0, dim, 2, dtype=jnp.float32) / dim)
            freqs = jnp.arange(seq_len, dtype=jnp.float32)[:, None] * inv_freq[None, :]
            emb = jnp.concatenate([freqs, freqs], axis=-1)
            return (jnp.sin(emb), jnp.cos(emb))

        def mala_attn(q, k, v):
            sin, cos = rope_sin_cos(q.shape[1], q.shape[-1])
            sin, cos = (sin[None, :, None, :], cos[None, :, None, :])
            q = q * cos + rotate_half(q) * sin
            k = k * cos + rotate_half(k) * sin
            scale = q.shape[-1] ** (-0.5)
            seq_len = q.shape[1]
            kv = jnp.einsum('bshd,bshe->bhde', k, v)
            ksum = k.sum(axis=1)
            vsum = v.sum(axis=1)
            num = jnp.einsum('bshd,bhde->bshe', q, kv) * scale + vsum[:, None, :, :]
            den = jnp.einsum('bshd,bhd->bsh', q, ksum) * scale + seq_len
            return num / den[..., None]

        def lepe_conv(v, w, b):
            Bb, Ss = (v.shape[0], v.shape[1])
            x = v.transpose(0, 2, 3, 1).reshape(Bb, H * DV, Ss)
            y = jax.lax.conv_general_dilated(x, w, window_strides=(1,), padding=[(KLEPE // 2, KLEPE // 2)], dimension_numbers=('NCH', 'OIH', 'NCH'), feature_group_count=H * DV)
            y = y + b[None, :, None]
            return y.reshape(Bb, H, DV, Ss).transpose(0, 3, 1, 2)
        key = jax.random.key(seed)
        ks = jax.random.split(key, 8)
        w = 0.02
        return {'hidden_states': jax.random.normal(ks[0], (B, S, D), dtype=jnp.float32), 'Wq': jax.random.normal(ks[1], (D, D), dtype=jnp.float32) * w, 'Wk': jax.random.normal(ks[2], (D, D), dtype=jnp.float32) * w, 'Wv': jax.random.normal(ks[3], (D, D), dtype=jnp.float32) * w, 'Wg': jax.random.normal(ks[4], (D, D), dtype=jnp.float32) * w, 'Wo': jax.random.normal(ks[5], (D, D), dtype=jnp.float32) * w, 'lepe_w': jax.random.normal(ks[6], (D, 1, KLEPE), dtype=jnp.float32) * 0.1, 'lepe_b': jnp.zeros((D,), dtype=jnp.float32)}
    _L0_attn_in = _L0_attn_setup()

    def _L0_ffn_setup():
        import jax, jax.numpy as jnp
        import numpy as np
        B, S, H = (2, 256, 128)
        E_ROUTED = 8
        TOP_K = 2
        I = 256
        key = jax.random.key(seed)
        ks = jax.random.split(key, 9)
        s = 0.02
        return {'x': jax.random.normal(ks[0], (B, S, H), dtype=jnp.float32), 'shared_gate': jax.random.normal(ks[1], (I, H), dtype=jnp.float32) * s, 'shared_up': jax.random.normal(ks[2], (I, H), dtype=jnp.float32) * s, 'shared_down': jax.random.normal(ks[3], (H, I), dtype=jnp.float32) * s, 'gate_w': jax.random.normal(ks[4], (E_ROUTED, H, I), dtype=jnp.float32) * s, 'up_w': jax.random.normal(ks[5], (E_ROUTED, H, I), dtype=jnp.float32) * s, 'down_w': jax.random.normal(ks[6], (E_ROUTED, I, H), dtype=jnp.float32) * s, 'router_w': jax.random.normal(ks[7], (E_ROUTED, H), dtype=jnp.float32) * s, 'routing_bias': jnp.zeros((E_ROUTED,), dtype=jnp.float32)}
    _L0_ffn_in = _L0_ffn_setup()
    _d = {'L0_attn_hidden_states': _L0_attn_in['hidden_states'], 'L0_attn_Wq': _L0_attn_in['Wq'], 'L0_attn_Wk': _L0_attn_in['Wk'], 'L0_attn_Wv': _L0_attn_in['Wv'], 'L0_attn_Wg': _L0_attn_in['Wg'], 'L0_attn_Wo': _L0_attn_in['Wo'], 'L0_attn_lepe_w': _L0_attn_in['lepe_w'], 'L0_attn_lepe_b': _L0_attn_in['lepe_b'], 'L0_ffn_shared_gate': _L0_ffn_in['shared_gate'], 'L0_ffn_shared_up': _L0_ffn_in['shared_up'], 'L0_ffn_shared_down': _L0_ffn_in['shared_down'], 'L0_ffn_gate_w': _L0_ffn_in['gate_w'], 'L0_ffn_up_w': _L0_ffn_in['up_w'], 'L0_ffn_down_w': _L0_ffn_in['down_w'], 'L0_ffn_router_w': _L0_ffn_in['router_w'], 'L0_ffn_routing_bias': _L0_ffn_in['routing_bias']}
    _x0 = _d['L0_attn_hidden_states']
    _d['L0_attn_hidden_states'] = jax.random.normal(jax.random.fold_in(jax.random.key(seed), 1), (8, 512, 128), dtype=_x0.dtype)
    del _x0
    return _d

def reference(L0_attn_hidden_states, L0_attn_Wq, L0_attn_Wk, L0_attn_Wv, L0_attn_Wg, L0_attn_Wo, L0_attn_lepe_w, L0_attn_lepe_b, L0_ffn_shared_gate, L0_ffn_shared_up, L0_ffn_shared_down, L0_ffn_gate_w, L0_ffn_up_w, L0_ffn_down_w, L0_ffn_router_w, L0_ffn_routing_bias):

    def _L0_attn_ref(hidden_states, Wq, Wk, Wv, Wg, Wo, lepe_w, lepe_b):
        import jax, jax.numpy as jnp
        import numpy as np
        B, S, D = (4, 512, 128)
        H = 8
        DK = D // H
        DV = D // H
        KLEPE = 5
        ROPE_BASE = 10000.0

        def rotate_half(x):
            x1, x2 = jnp.split(x, 2, axis=-1)
            return jnp.concatenate([-x2, x1], axis=-1)

        def rope_sin_cos(seq_len, dim):
            inv_freq = 1.0 / ROPE_BASE ** (jnp.arange(0, dim, 2, dtype=jnp.float32) / dim)
            freqs = jnp.arange(seq_len, dtype=jnp.float32)[:, None] * inv_freq[None, :]
            emb = jnp.concatenate([freqs, freqs], axis=-1)
            return (jnp.sin(emb), jnp.cos(emb))

        def mala_attn(q, k, v):
            sin, cos = rope_sin_cos(q.shape[1], q.shape[-1])
            sin, cos = (sin[None, :, None, :], cos[None, :, None, :])
            q = q * cos + rotate_half(q) * sin
            k = k * cos + rotate_half(k) * sin
            scale = q.shape[-1] ** (-0.5)
            seq_len = q.shape[1]
            kv = jnp.einsum('bshd,bshe->bhde', k, v)
            ksum = k.sum(axis=1)
            vsum = v.sum(axis=1)
            num = jnp.einsum('bshd,bhde->bshe', q, kv) * scale + vsum[:, None, :, :]
            den = jnp.einsum('bshd,bhd->bsh', q, ksum) * scale + seq_len
            return num / den[..., None]

        def lepe_conv(v, w, b):
            Bb, Ss = (v.shape[0], v.shape[1])
            x = v.transpose(0, 2, 3, 1).reshape(Bb, H * DV, Ss)
            y = jax.lax.conv_general_dilated(x, w, window_strides=(1,), padding=[(KLEPE // 2, KLEPE // 2)], dimension_numbers=('NCH', 'OIH', 'NCH'), feature_group_count=H * DV)
            y = y + b[None, :, None]
            return y.reshape(Bb, H, DV, Ss).transpose(0, 3, 1, 2)
        Bb, Ss, _ = hidden_states.shape
        q = (hidden_states @ Wq.T).reshape(Bb, Ss, H, DK)
        k = (hidden_states @ Wk.T).reshape(Bb, Ss, H, DK)
        v = (hidden_states @ Wv.T).reshape(Bb, Ss, H, DV)
        o_gate = hidden_states @ Wg.T
        o = mala_attn(q, k, v) + lepe_conv(v, lepe_w, lepe_b)
        o = o.reshape(Bb, Ss, H * DV) * o_gate
        return o @ Wo.T

    def _L0_ffn_ref(x, shared_gate, shared_up, shared_down, gate_w, up_w, down_w, router_w, routing_bias):
        import jax, jax.numpy as jnp
        import numpy as np
        B, S, H = (2, 256, 128)
        E_ROUTED = 8
        TOP_K = 2
        I = 256
        b, s, h = x.shape
        shared = jnp.einsum('bsi,hi->bsh', jax.nn.silu(jnp.einsum('bsh,ih->bsi', x, shared_gate)) * jnp.einsum('bsh,ih->bsi', x, shared_up), shared_down)
        logits = jnp.einsum('bsh,eh->bse', x, router_w) + routing_bias
        probs = jax.nn.sigmoid(logits)
        scores, indices = jax.lax.top_k(probs, TOP_K)
        scores = scores / jnp.sum(scores, axis=-1, keepdims=True)
        t = b * s
        xf = x.reshape(t, h)
        idx = indices.reshape(t, TOP_K)
        sc = scores.reshape(t, TOP_K)
        w = jnp.zeros((t, E_ROUTED), dtype=x.dtype)
        w = w.at[jnp.arange(t)[:, None], idx].add(sc)
        g = jax.nn.silu(jnp.einsum('th,ehi->tei', xf, gate_w))
        u = jnp.einsum('th,ehi->tei', xf, up_w)
        combined = jnp.einsum('tei,eih,te->th', g * u, down_w, w)
        return shared + combined.reshape(b, s, h)
    x = L0_attn_hidden_states
    x = x + 0.5 * _L0_ffn_ref(_layernorm(x, axis=-1), L0_ffn_shared_gate, L0_ffn_shared_up, L0_ffn_shared_down, L0_ffn_gate_w, L0_ffn_up_w, L0_ffn_down_w, L0_ffn_router_w, L0_ffn_routing_bias)
    x = x + _L0_attn_ref(_layernorm(x, axis=-1), L0_attn_Wq, L0_attn_Wk, L0_attn_Wv, L0_attn_Wg, L0_attn_Wo, L0_attn_lepe_w, L0_attn_lepe_b)
    x = x + 0.5 * _L0_ffn_ref(_layernorm(x, axis=-1), L0_ffn_shared_gate, L0_ffn_shared_up, L0_ffn_shared_down, L0_ffn_gate_w, L0_ffn_up_w, L0_ffn_down_w, L0_ffn_router_w, L0_ffn_routing_bias)
    return x

_drawn_inputs = setup_inputs


def setup_inputs(seed=0):
    import zlib

    import numpy as np

    out = dict(_drawn_inputs(seed))
    spreads = {'L0_attn_lepe_b': (0.0, 0.8), 'L0_ffn_routing_bias': (0.0, 0.8)}
    factors = {'L0_attn_Wq': 8.0,
     'L0_attn_Wk': 8.0,
     'L0_attn_Wv': 8.0,
     'L0_attn_Wg': 8.0,
     'L0_attn_Wo': 8.0,
     'L0_attn_lepe_w': 8.0,
     'L0_ffn_shared_gate': 6.647,
     'L0_ffn_shared_up': 6.455,
     'L0_ffn_shared_down': 6.398,
     'L0_ffn_gate_w': 8.0,
     'L0_ffn_up_w': 8.0,
     'L0_ffn_down_w': 8.0,
     'L0_ffn_router_w': 8.0}
    for name, (base, spread) in spreads.items():
        noise = np.random.default_rng([zlib.crc32(name.encode()), seed]).standard_normal(out[name].shape)
        drawn = base * np.exp(spread * noise) if base else spread * noise
        out[name] = jnp.asarray(drawn.astype(out[name].dtype))
    for name, factor in factors.items():
        out[name] = (out[name] * factor).astype(out[name].dtype)
    return out
```

```python
from contextlib import ExitStack

import numpy as np
import concourse.bass as bass
from concourse import mybir

P = 128
ALU = mybir.AluOpType
ACT = mybir.ActivationFunctionType
AX = mybir.AxisListType
F32 = mybir.dt.float32
F32R = mybir.dt.float32r
I32 = mybir.dt.int32

B, S, D = 8, 512, 128
T = S // P
NH, DK = 8, 16
E = 8
NE = E + 1
I = 256
HALVES = I // P
STEPS = NE * HALVES
ROUTED = E * HALVES
TAPS = 5
PAD = TAPS // 2
HR = 6
WD = 4
VW = D + 2
LAG = 4
EPS = 1e-5
RSQRT_MAGIC = 0x5F3759DF
NEWTON = 3
LN_LINKS = 5 + 3 * NEWTON
ROUTE_LINKS = 12


def build(nc, x, wq, wqp, wk, wv, wg, wo, lepe_w, lepe_b, sgate, sup, sdown, gate_w, up_w, down_w,
          router, rbias, cos_f, sin_f, cos_t, sin_t, blockmask, headmask, expand, tri, ident_in, out):
    with ExitStack() as ctx:
        def sb(name, shape, dt=F32):
            return ctx.enter_context(nc.sbuf_tensor(name, shape, dt))

        def ps(name):
            return ctx.enter_context(nc.psum_tensor(name, [P, 512], F32))

        def sem(name):
            return ctx.enter_context(nc.semaphore(name))

        gate_ps = [ps(f"gate_ps{i}") for i in range(2)]
        up_ps = [ps(f"up_ps{i}") for i in range(3)]
        down_ps = ps("down_ps")
        misc = [ps(f"misc{i}") for i in range(2)]

        EW = 3 * I
        raw = sb("raw_weights", [P, 3, EW])
        w_hi = sb("w_hi", [P, NE, EW], F32R)
        w_lo = sb("w_lo", [P, NE, EW], F32R)
        NA = 5
        raw_attn = sb("raw_attn", [P, NA * D + E])
        aw_hi = sb("aw_hi", [P, NA * D + E], F32R)
        aw_lo = sb("aw_lo", [P, NA * D + E], F32R)
        Q, QP, K, V, G = [slice(i * D, (i + 1) * D) for i in range(NA)]
        R = slice(NA * D, NA * D + E)
        wo_sb = sb("wo_sb", [P, D])
        taps = sb("taps", [P, TAPS])
        tap_bias = sb("tap_bias", [P, 1])
        rbias_sb = sb("rbias_sb", [P, E])
        cosf = sb("cosf", [P, S])
        sinf = sb("sinf", [P, S])
        cost = sb("cost", [P, T, DK])
        sint = sb("sint", [P, T, DK])
        bmask = sb("bmask", [P, D])
        hmask = sb("hmask", [P, NH])
        expd = sb("expd", [T * NH, T, D])
        tri_sb = sb("tri_sb", [P, E, E])
        ident = sb("ident", [P, P])
        x_ln = sb("x_ln", [P, T, D])
        x_res = sb("x_res", [P, T, D])
        x1 = sb("x1", [P, T, D])
        x2 = sb("x2", [P, T, D])
        x3 = sb("x3", [P, T, D])
        xn = {l: sb(f"xn{l}", [P, T, D]) for l in (1, 2, 3)}
        xt_hi = {l: sb(f"xt_hi{l}", [P, S], F32R) for l in (1, 2, 3)}
        xt_lo = {l: sb(f"xt_lo{l}", [P, S], F32R) for l in (1, 2, 3)}
        stats = sb("stats", [P, T, 6])
        mv = sb("mv", [P, T, 2])
        ve = sb("ve", [P, T])
        vh = sb("vh", [P, T])
        nt = sb("nt", [P, T])
        rstd = sb("rstd", [P, T])
        lg = {l: sb(f"lg{l}", [P, T, E]) for l in (1, 3)}
        lneg = {l: sb(f"lneg{l}", [P, T, E]) for l in (1, 3)}
        lpos = {l: sb(f"lpos{l}", [P, T, E]) for l in (1, 3)}
        rt = {l: sb(f"rt{l}", [P, 3, T, E]) for l in (1, 3)}
        pr = {l: sb(f"pr{l}", [P, T, E]) for l in (1, 3)}
        beats = sb("beats", [P, T, E, E])
        ties = sb("ties", [P, T, E, E])
        rank = sb("rank", [P, T, E])
        top = sb("top", [P, T])
        wtok = {l: sb(f"wtok{l}", [P, E, T]) for l in (1, 3)}
        wT = {l: sb(f"wT{l}", [T * E, P]) for l in (1, 3)}
        w_bc = {l: sb(f"w_bc{l}", [P, E, S]) for l in (1, 3)}
        g = sb("g", [P, 3, S])
        gw = sb("gw", [P, 3, S])
        h = sb("h", [P, 2, S])
        h_hi = sb("h_hi", [P, HR, S], F32R)
        h_lo = sb("h_lo", [P, HR, S], F32R)
        yT = sb("yT", [P, S])
        qc = sb("qc", [P, S])
        qs = sb("qs", [P, S])
        q_rot = sb("q_rot", [P, S])
        kc = sb("kc", [P, T, D])
        ks_ = sb("ks", [P, T, D])
        k_rot = sb("k_rot", [P, T, D])
        v_tok = sb("v_tok", [P, T, VW])
        vT = sb("vT", [P, S + 2 * PAD])
        vsum = sb("vsum", [P, 1])
        ogate = sb("ogate", [P, S])
        kv_bd = sb("kv_bd", [P, D])
        ks_bd = sb("ks_bd", [P, NH])
        den = sb("den", [P, T * NH])
        rden = sb("rden", [P, T * NH])
        rdenT = sb("rdenT", [T * NH, P])
        rden_bc = sb("rden_bc", [P, S])
        spare = raw[:].rearrange("p r n -> p (r n)")
        conv = spare[:, 0:2 * S].rearrange("p (b n) -> p b n", b=2)
        att = spare[:, 2 * S:3 * S]
        oT = spare[:, 3 * S:4 * S]

        w_dram = {l: nc.dram_tensor(f"w_scratch{l}", [B, T * E, P], F32).ap() for l in (1, 3)}

        w_loaded = [sem(f"w_loaded{i}") for i in range(3)]
        attn_loaded, const_loaded, ident_loaded = sem("attn_loaded"), sem("const_loaded"), sem("ident_loaded")
        x_ln_loaded, x_res_loaded = sem("x_ln_loaded"), sem("x_res_loaded")
        w_hi_done, w_lo_done, attn_hi_done, attn_lo_done = sem("w_hi_done"), sem("w_lo_done"), sem("attn_hi_done"), sem("attn_lo_done")
        pads_set = sem("pads_set")
        gate_ready, up_ready, silu_done, gw_done = sem("gate_ready"), sem("up_ready"), sem("silu_done"), sem("gw_done")
        h_done, hi_done, lo_done, down_done = sem("h_done"), sem("hi_done"), sem("lo_done"), sem("down_done")
        acc_copied = sem("acc_copied")
        ln_link = {l: sem(f"ln_link{l}") for l in (1, 2, 3)}
        xn_done = {l: sem(f"xn_done{l}") for l in (1, 2, 3)}
        xnT_ready = {l: sem(f"xnT_ready{l}") for l in (1, 2, 3)}
        xt_hi_done = {l: sem(f"xt_hi_done{l}") for l in (1, 2, 3)}
        xt_lo_done = {l: sem(f"xt_lo_done{l}") for l in (1, 2, 3)}
        logits_ready = {l: sem(f"logits_ready{l}") for l in (1, 3)}
        clamped = {l: sem(f"clamped{l}") for l in (1, 3)}
        sig_done = {l: sem(f"sig_done{l}") for l in (1, 3)}
        route_link = {l: sem(f"route_link{l}") for l in (1, 3)}
        wtok_done = {l: sem(f"wtok_done{l}") for l in (1, 3)}
        wT_ready = {l: sem(f"wT_ready{l}") for l in (1, 3)}
        wT_copied = {l: sem(f"wT_copied{l}") for l in (1, 3)}
        w_stored = {l: sem(f"w_stored{l}") for l in (1, 3)}
        w_bc_loaded = {l: [sem(f"w_bc_loaded{l}_{i}") for i in range(WD)] for l in (1, 3)}
        y_tok_ready = {l: sem(f"y_tok_ready{l}") for l in (1, 3)}
        x1_done, x2_done, x3_done, x3_free = sem("x1_done"), sem("x2_done"), sem("x3_done"), sem("x3_free")
        q_ready, qp_ready, k_ready, vT_ready, v_ready, og_ready = (sem(n) for n in (
            "q_ready", "qp_ready", "k_ready", "vT_ready", "v_ready", "og_ready"))
        q_cos_done, q_sin_done, q_rot_done = sem("q_cos_done"), sem("q_sin_done"), sem("q_rot_done")
        k_parts_done, k_rot_done = sem("k_parts_done"), sem("k_rot_done")
        vT_done, v_tok_done, og_done = sem("vT_done"), sem("v_tok_done"), sem("og_done")
        kv_ready, kv_bd_done, den_ready, den_link = sem("kv_ready"), sem("kv_bd_done"), sem("den_ready"), sem("den_link")
        rden_done, rdenT_ready, rdenT_done, rbc_ready, rbc_done = (sem(n) for n in (
            "rden_done", "rdenT_ready", "rdenT_done", "rbc_ready", "rbc_done"))
        conv0_done, conv_link, num_ready, att_done = sem("conv0_done"), sem("conv_link"), sem("num_ready"), sem("att_done")
        o_sum_done, oT_done, proj_ready = sem("o_sum_done"), sem("oT_done"), sem("proj_ready")

        def wait(eng, s, value):
            if not isinstance(value, int) or value > 0:
                eng.wait_ge(s, value)

        def F1(c):
            return 1, c, (0 if isinstance(c, int) and c == 0 else 2 * c - 1)

        def F2(c):
            return 3, c, (2 * B - 1 if isinstance(c, int) and c == B - 1 else 2 * c + 2)

        def count(p, k):
            return p[2] * STEPS + k + 1

        def run_phase(pieces, cur, prev, front, back, back_lag):
            for k in range(STEPS):
                if cur:
                    front(cur, k)
                j = k - back_lag
                if back and j >= 0 and cur:
                    back(cur, j)
                if back and j < 0 and prev:
                    back(prev, STEPS + j)
                for piece in pieces.get(k, ()):
                    piece()

        block = ctx.enter_context(nc.Block())

        @block.sync
        def _(sp):
            def load_x_ln(c):
                wait(sp, xn_done[1], c)
                sp.dma_start(x_ln[:], x[c].rearrange("(t p) d -> p t d", p=P)).then_inc(x_ln_loaded, 16)

            def load_x_res(c):
                wait(sp, x1_done, c)
                sp.dma_start(x_res[:], x[c].rearrange("(t p) d -> p t d", p=P)).then_inc(x_res_loaded, 16)

            def spread_weights(l, c, p_before):
                wait(sp, wT_copied[l], c + 1)
                sp.dma_start(w_dram[l][c], wT[l][:]).then_inc(w_stored[l], 16)
                wait(sp, w_stored[l], 16 * c + 16)
                if p_before is not None:
                    wait(sp, gw_done, p_before[2] * ROUTED + ROUTED)
                rows = T * E // WD
                for i in range(WD):
                    sp.dma_start(w_bc[l][:, i * E // WD:(i + 1) * E // WD].rearrange("p e n -> p (e n)"),
                                 w_dram[l][c, i * rows:(i + 1) * rows].rearrange("(o r) n -> o (r n)", o=1)
                                 .to_broadcast([P, rows * P])).then_inc(w_bc_loaded[l][i], 16)

            def store(c):
                wait(sp, x3_done, c + 1)
                sp.dma_start(out[c].rearrange("(t p) d -> p t d", p=P), x3[:]).then_inc(x3_free, 16)

            sp.sem_inc(x3_free, 16)
            load_x_ln(0)
            sp.dma_start(ident[:], ident_in).then_inc(ident_loaded, 16)
            for o, w in enumerate((wq, wqp, wk, wv, wg)):
                sp.dma_start(raw_attn[:, o * D:(o + 1) * D], w).then_inc(attn_loaded, 16)
            sp.dma_start(raw_attn[:, R], router).then_inc(attn_loaded, 16)
            sp.dma_start(rbias_sb[:], rbias.rearrange("(o e) -> o e", o=1).to_broadcast([P, E])).then_inc(ident_loaded, 16)
            sp.dma_start(tri_sb[:].rearrange("p e j -> p (e j)"), tri.to_broadcast([P, E * E])).then_inc(ident_loaded, 16)
            for e in range(NE):
                wait(sp, w_lo_done, e - 2)
                r = raw[:, e % 3]
                gs, us, ds = (sgate, sup, sdown) if e == 0 else (gate_w[e - 1], up_w[e - 1], down_w[e - 1])
                sp.dma_start(r[:, 0:I], gs).then_inc(w_loaded[e % 3], 16)
                sp.dma_start(r[:, I:2 * I], us).then_inc(w_loaded[e % 3], 16)
                sp.dma_start(r[:, 2 * I:].rearrange("p (s d) -> p s d", s=HALVES),
                             ds.rearrange("(s p) d -> p s d", p=P)).then_inc(w_loaded[e % 3], 16)
                if e == 1:
                    for dst, src in ((wo_sb[:], wo), (taps[:], lepe_w.rearrange("d o k -> d (o k)")),
                                     (tap_bias[:], lepe_b.rearrange("(d o) -> d o", o=1)),
                                     (cosf[:], cos_f), (sinf[:], sin_f),
                                     (cost[:], cos_t.rearrange("(t p) d -> p t d", p=P)),
                                     (sint[:], sin_t.rearrange("(t p) d -> p t d", p=P)),
                                     (bmask[:], blockmask), (hmask[:], headmask), (expd[:], expand)):
                        sp.dma_start(dst, src).then_inc(const_loaded, 16)
                if e == 2:
                    spread_weights(1, 0, None)
            load_x_res(0)
            load_x_ln(1)
            spread_weights(1, 1, F1(0))
            load_x_res(1)
            load_x_ln(2)
            spread_weights(3, 0, None)

            def middle(i, last):
                spread_weights(1, i + 1, F1(i))
                load_x_res(i + 1)
                if not last:
                    load_x_ln(i + 2)
                store(i - 1)
                spread_weights(3, i, F2(i - 1))
            with sp.Fori(1, B - 2) as i:
                middle(i, False)
            middle(B - 2, True)
            store(B - 2)
            spread_weights(3, B - 1, F2(B - 2))
            store(B - 1)
            sp.wait_ge(x3_free, 16 * B + 16)

        @block.tensor
        def _(pe):
            def product3(dst, w_h, w_l, m_h, m_l, start, stop):
                pe.matmul(dst, w_h, m_h, start=start, stop=False)
                pe.matmul(dst, w_l, m_h, start=False, stop=False)
                return pe.matmul(dst, w_h, m_l, start=False, stop=stop)

            def gate_up(p, k):
                l, c, _ = p
                n, e, half = count(p, k), k // HALVES, k % HALVES
                if k == 0:
                    pe.wait_ge(xt_lo_done[l], c + 1)
                if isinstance(p[2], int) and p[2] == 0 and half == 0:
                    pe.wait_ge(w_lo_done, e + 1)
                wait(pe, silu_done, n - 2)
                at = slice(half * P, half * P + P)
                product3(gate_ps[k % 2][:], w_hi[:, e, at], w_lo[:, e, at], xt_hi[l][:], xt_lo[l][:],
                         True, True).then_inc(gate_ready, 1)
                wait(pe, h_done, n - 3)
                at = slice(I + half * P, I + half * P + P)
                product3(up_ps[k % 3][:], w_hi[:, e, at], w_lo[:, e, at], xt_hi[l][:], xt_lo[l][:],
                         True, True).then_inc(up_ready, 1)

            def down(p, k):
                n, e, half = count(p, k), k // HALVES, k % HALVES
                pe.wait_ge(lo_done, n)
                if k == 0:
                    wait(pe, acc_copied, p[2])
                at = slice(2 * I + half * D, 2 * I + half * D + D)
                product3(down_ps[:], w_hi[:, e, at], w_lo[:, e, at], h_hi[:, k % HR, :], h_lo[:, k % HR, :],
                         k == 0, k == STEPS - 1).then_inc(down_done, 1)

            def turn(l, src, ready, value, bank, free, done):
                def piece():
                    pe.wait_ge(ready, value)
                    for s, v in free:
                        wait(pe, s, v)
                    for t in range(T):
                        mm = pe.transpose(bank[:, t * P:(t + 1) * P], src(t), ident[:])
                    mm.then_inc(done, 1)
                return piece

            def xn_turn(l, c, bank, *free):
                return turn(l, lambda t: xn[l][:, t, :], xn_done[l], c + 1, bank, free, xnT_ready[l])

            def y_turn(l, p, bank, *free):
                return turn(l, lambda t: yT[:, t * P:(t + 1) * P], acc_copied, p[2] + 1, bank, free,
                            y_tok_ready[l])

            def logits(l, c, bank, *free):
                def piece():
                    pe.wait_ge(xt_lo_done[l], c + 1)
                    for s, v in free:
                        wait(pe, s, v)
                    for t in range(T):
                        tile = slice(t * P, (t + 1) * P)
                        mm = product3(bank[:, t * E:(t + 1) * E], xt_hi[l][:, tile], xt_lo[l][:, tile],
                                      aw_hi[:, R], aw_lo[:, R], True, True)
                    mm.then_inc(logits_ready[l], 1)
                return piece

            def w_turn(l, c, bank, *free):
                def piece():
                    pe.wait_ge(wtok_done[l], c + 1)
                    for s, v in free:
                        wait(pe, s, v)
                    pe.transpose(bank[0:T * E, 0:P], wtok[l][:].rearrange("p e t -> p (e t)"),
                                 ident[:]).then_inc(wT_ready[l], 1)
                return piece

            def project(c, w, bank, done, *free):
                def piece():
                    pe.wait_ge(xt_lo_done[2], c + 1)
                    for s, v in free:
                        wait(pe, s, v)
                    product3(bank[:], aw_hi[:, w], aw_lo[:, w], xt_hi[2][:], xt_lo[2][:],
                             True, True).then_inc(done, 1)
                return piece

            def project_tokens(c, w, bank, done, *free):
                def piece():
                    pe.wait_ge(xt_lo_done[2], c + 1)
                    for s, v in free:
                        wait(pe, s, v)
                    for t in range(T):
                        tile = slice(t * P, (t + 1) * P)
                        mm = product3(bank[:, t * D:(t + 1) * D], xt_hi[2][:, tile], xt_lo[2][:, tile],
                                      aw_hi[:, w], aw_lo[:, w], True, True)
                    mm.then_inc(done, 1)
                return piece

            def kv(c, bank, *free):
                def piece():
                    pe.wait_ge(k_rot_done, c + 1)
                    pe.wait_ge(v_tok_done, c + 1)
                    for s, v in free:
                        wait(pe, s, v)
                    for t in range(T):
                        mm = pe.matmul(bank[:, 0:VW], k_rot[:, t, :], v_tok[:, t, :], start=t == 0, stop=t == T - 1)
                    mm.then_inc(kv_ready, 1)
                return piece

            def denominators(c, bank, *free):
                def piece():
                    pe.wait_ge(kv_bd_done, c + 1)
                    pe.wait_ge(q_rot_done, c + 1)
                    for s, v in free:
                        wait(pe, s, v)
                    for t in range(T):
                        mm = pe.matmul(bank[:, t * NH:(t + 1) * NH], q_rot[:, t * P:(t + 1) * P], ks_bd[:],
                                       start=True, stop=True)
                    mm.then_inc(den_ready, 1)
                return piece

            def rden_turn(c, bank, *free):
                def piece():
                    pe.wait_ge(rden_done, c + 1)
                    for s, v in free:
                        wait(pe, s, v)
                    pe.transpose(bank[0:T * NH, 0:P], rden[:], ident[:]).then_inc(rdenT_ready, 1)
                return piece

            def rden_spread(c, bank, *free):
                def piece():
                    pe.wait_ge(rdenT_done, c + 1)
                    for s, v in free:
                        wait(pe, s, v)
                    for t in range(T):
                        mm = pe.matmul(bank[:, t * P:(t + 1) * P], expd[:, t, :], rdenT[:], start=True, stop=True)
                    mm.then_inc(rbc_ready, 1)
                return piece

            def numerators(c, bank, *free):
                def piece():
                    pe.wait_ge(kv_bd_done, c + 1)
                    pe.wait_ge(q_rot_done, c + 1)
                    for s, v in free:
                        wait(pe, s, v)
                    pe.matmul(bank[:], kv_bd[:], q_rot[:], start=True, stop=True).then_inc(num_ready, 1)
                return piece

            def out_project(c, bank, *free):
                def piece():
                    pe.wait_ge(oT_done, c + 1)
                    for s, v in free:
                        wait(pe, s, v)
                    for t in range(T):
                        mm = pe.matmul(bank[:, t * D:(t + 1) * D], oT[:, t * P:(t + 1) * P], wo_sb[:],
                                       start=True, stop=True)
                    mm.then_inc(proj_ready, 1)
                return piece

            m0, m1 = misc

            def prep1(n, a):
                return (xn_turn(1, n, m1, (wT_copied[3], a + 1)),
                        logits(1, n, m0, (clamped[3], a + 1)),
                        w_turn(1, n, m1, (q_sin_done, n)))

            def attn1(c, prev1, prev0, before_v):
                return (y_turn(1, F1(c), m1, prev1),
                        xn_turn(2, c, m1, (x1_done, c + 1)),
                        project(c, Q, m0, q_ready, prev0),
                        project(c, QP, m1, qp_ready, (xt_lo_done[2], c + 1)),
                        project_tokens(c, K, m0, k_ready, (q_cos_done, c + 1)),
                        project(c, V, m1, vT_ready, (q_sin_done, c + 1), *before_v),
                        project_tokens(c, V, m0, v_ready, (k_parts_done, c + 1)),
                        project(c, G, m1, og_ready, (vT_done, c + 1)))

            def attn2(c):
                return (kv(c, m0, (v_tok_done, c + 1)),
                        denominators(c, m1, (og_done, c + 1)),
                        rden_turn(c, m0, (kv_bd_done, c + 1)),
                        rden_spread(c, m1, (den_link, c + 1)),
                        numerators(c, m0, (rdenT_done, c + 1)),
                        out_project(c, m0, (att_done, c + 1)),
                        xn_turn(3, c, m1, (rbc_done, c + 1), (x3_done, c)),
                        logits(3, c, m0, (x2_done, c + 1)),
                        w_turn(3, c, m1, (xt_lo_done[3], c + 1)))

            def phase_a(i, cur, prev, o):
                a = attn2(i - 1)
                at = {0: a[0:1], 1: a[1:2], 3: a[2:3], 4: a[3:5], 7: a[5:6],
                      11: a[6:7], 13: a[7:8], 17: a[8:9]}
                if o is not None:
                    at[6] = (y_turn(3, F2(o), m1, (rbc_done, i)),)
                run_phase(at, cur, prev, gate_up, down, LAG)

            def phase_b(i, cur, prev, n):
                prev1 = (xt_lo_done[1], i + 2) if n is not None else (wT_copied[3], i)
                prev0 = (clamped[1], i + 2) if n is not None else (clamped[3], i)
                c = attn1(i, prev1, prev0, ((wT_copied[1], i + 2),) if n is not None else ())
                at = {5: c[0:1], 10: c[1:2], 12: c[2:3], 13: c[3:4], 14: c[4:5], 16: c[5:7], 17: c[7:8]}
                if n is not None:
                    r = prep1(n, i - 1)
                    at[3], at[5], at[15] = r[0:1], at[5] + r[1:2], r[2:3]
                run_phase(at, cur, prev, gate_up, down, LAG)

            pe.wait_ge(ident_loaded, 48)
            xn_turn(1, 0, m1)()
            pe.wait_ge(attn_lo_done, 1)
            logits(1, 0, m0)()
            w_turn(1, 0, m1)()
            run_phase({}, F1(0), None, gate_up, down, LAG)
            pe.wait_ge(const_loaded, 160)
            phase_b(0, None, F1(0), 1)
            phase_a(1, F1(1), None, None)
            with pe.Fori(1, B - 1) as i:
                phase_b(i, F2(i - 1), F1(i), i + 1)
                phase_a(i + 1, F1(i + 1), F2(i - 1), i - 1)
            phase_b(B - 1, F2(B - 2), F1(B - 1), None)
            phase_a(B, None, F2(B - 2), B - 2)
            run_phase({}, F2(B - 1), None, gate_up, down, LAG)
            run_phase({}, None, F2(B - 1), gate_up, down, LAG)
            y_turn(3, F2(B - 1), m1, (wT_copied[3], B))()

        @block.scalar
        def _(act):
            def silu(p, k):
                n = count(p, k)
                act.wait_ge(gate_ready, n)
                wait(act, h_done, n - 3)
                nc.scalar.activation(g[:, k % 3, :], gate_ps[k % 2][:], ACT.Silu).then_inc(silu_done, 1)

            def round_h(p, k):
                n = count(p, k)
                act.wait_ge(h_done, n)
                wait(act, down_done, n - HR)
                nc.scalar.activation(h_hi[:, k % HR, :], h[:, k % 2, :], ACT.Copy).then_inc(hi_done, 1)

            def copy(dst, src, ready, value, done, *free):
                def piece():
                    act.wait_ge(ready, value)
                    for s, v in free:
                        wait(act, s, v)
                    nc.scalar.activation(dst, src, ACT.Copy).then_inc(done, 1)
                return piece

            def copy_out(p, l):
                return copy(yT[:], down_ps[:], down_done, p[2] * STEPS + STEPS, acc_copied)

            def round_xn(l, c, bank, *free):
                return copy(xt_hi[l][:], bank[:], xnT_ready[l], c + 1, xt_hi_done[l], *free)

            def sigmoids(l, c):
                def piece():
                    act.wait_ge(clamped[l], c + 1)
                    nc.scalar.activation(rt[l][:, 0], lneg[l][:], ACT.Silu)
                    nc.scalar.activation(rt[l][:, 1], lpos[l][:], ACT.Tanh, scale=0.5).then_inc(sig_done[l], 1)
                return piece

            def copy_wT(l, c, bank):
                return copy(wT[l][:], bank[0:T * E, 0:P], wT_ready[l], c + 1, wT_copied[l],
                            (w_stored[l], 16 * c))

            def values_T(c):
                def piece():
                    act.wait_ge(vT_ready, c + 1)
                    wait(act, conv_link, 4 * c)
                    wait(act, att_done, c)
                    nc.scalar.activation(vT[:, PAD:PAD + S], misc[1][:], ACT.Copy,
                                         accum_out=vsum[:]).then_inc(vT_done, 1)
                return piece

            def values_tok(c):
                return copy(v_tok[:, :, 0:D], misc[0][:].rearrange("p (t d) -> p t d", t=T), v_ready, c + 1,
                            v_tok_done, (kv_ready, c))

            def first_tap(c):
                def piece():
                    act.wait_ge(vT_done, c + 1)
                    wait(act, o_sum_done, c)
                    nc.scalar.activation(conv[:, 0, :], vT[:, 0:S], ACT.Identity, bias=tap_bias[:, 0:1],
                                         scale=taps[:, 0:1]).then_inc(conv0_done, 1)
                return piece

            def phase_a(i, cur, prev, o):
                c = i - 1
                at = {0: (copy(ogate[:], misc[1][:], og_ready, c + 1, og_done, (oT_done, c)), first_tap(c)),
                      3: (copy(rdenT[:], misc[0][0:T * NH, 0:P], rdenT_ready, c + 1, rdenT_done),),
                      5: (copy(rden_bc[:], misc[1][:], rbc_ready, c + 1, rbc_done),),
                      11: (round_xn(3, c, misc[1]),),
                      14: (sigmoids(3, c),), 17: (copy_wT(3, c, misc[1]),)}
                if o is not None:
                    at[4] = (copy_out(F2(o), 3),)
                run_phase(at, cur, prev, silu, round_h, 1)

            def phase_b(i, cur, prev, n):
                at = {4: (copy_out(F1(i), 1),), 10: (round_xn(2, i, misc[1]),), 16: (values_T(i),),
                      17: (values_tok(i),)}
                if n is not None:
                    at[3] = (round_xn(1, n, misc[1]),)
                    at[6] = (sigmoids(1, n),)
                    at[15] = (copy_wT(1, n, misc[1]),)
                run_phase(at, cur, prev, silu, round_h, 1)

            def cut_weights(e):
                act.wait_ge(w_loaded[e % 3], 48 * (e // 3 + 1))
                nc.scalar.activation(w_hi[:, e], raw[:, e % 3], ACT.Copy).then_inc(w_hi_done, 1)

            act.wait_ge(attn_loaded, 96)
            nc.scalar.activation(aw_hi[:], raw_attn[:], ACT.Copy).then_inc(attn_hi_done, 1)
            round_xn(1, 0, misc[1])()
            cut_weights(0)
            cut_weights(1)
            sigmoids(1, 0)()
            cut_weights(2)
            copy_wT(1, 0, misc[1])()
            for e in range(3, NE):
                cut_weights(e)
            run_phase({}, F1(0), None, silu, round_h, 1)
            act.wait_ge(const_loaded, 160)
            phase_b(0, None, F1(0), 1)
            phase_a(1, F1(1), None, None)
            with act.Fori(1, B - 1) as i:
                phase_b(i, F2(i - 1), F1(i), i + 1)
                phase_a(i + 1, F1(i + 1), F2(i - 1), i - 1)
            phase_b(B - 1, F2(B - 2), F1(B - 1), None)
            phase_a(B, None, F2(B - 2), B - 2)
            run_phase({}, F2(B - 1), None, silu, round_h, 1)
            run_phase({}, None, F2(B - 1), silu, round_h, 1)
            copy_out(F2(B - 1), 3)()

        @block.gpsimd
        def _(pool):
            def weigh(p, k):
                l, c, before = p
                n, e = count(p, k), k // HALVES - 1
                if e < 0:
                    return
                if k % HALVES == 0 and e % (E // WD) == 0:
                    pool.wait_ge(w_bc_loaded[l][e * WD // E], 16 * c + 16)
                pool.wait_ge(silu_done, n)
                wait(pool, h_done, n - 3)
                nc.gpsimd.tensor_tensor(gw[:, k % 3, :], g[:, k % 3, :], w_bc[l][:, e, :], ALU.mult).then_inc(gw_done, 1)

            def add_q(c):
                def piece():
                    pool.wait_ge(q_cos_done, c + 1)
                    pool.wait_ge(q_sin_done, c + 1)
                    wait(pool, num_ready, c)
                    nc.gpsimd.tensor_tensor(q_rot[:], qc[:], qs[:], ALU.add).then_inc(q_rot_done, 1)
                return piece

            def add_k(c):
                def piece():
                    pool.wait_ge(k_parts_done, c + 1)
                    wait(pool, kv_ready, c)
                    nc.gpsimd.tensor_tensor(k_rot[:], kc[:], ks_[:], ALU.add).then_inc(k_rot_done, 1)
                return piece

            def phase_a(i, cur, prev, o):
                run_phase({}, cur, prev, weigh, None, 0)

            def phase_b(i, cur, prev, n):
                run_phase({15: (add_q(i),), 16: (add_k(i),)}, cur, prev, weigh, None, 0)

            nc.gpsimd.memset(vT[:], 0.0)
            nc.gpsimd.memset(v_tok[:], 1.0).then_inc(pads_set, 1)
            run_phase({}, F1(0), None, weigh, None, 0)
            phase_b(0, None, F1(0), 1)
            phase_a(1, F1(1), None, None)
            with pool.Fori(1, B - 1) as i:
                phase_b(i, F2(i - 1), F1(i), i + 1)
                phase_a(i + 1, F1(i + 1), F2(i - 1), i - 1)
            phase_b(B - 1, F2(B - 2), F1(B - 1), None)
            phase_a(B, None, F2(B - 2), B - 2)
            run_phase({}, F2(B - 1), None, weigh, None, 0)

        @block.vector
        def _(dve):
            v = nc.vector

            class Links:
                def __init__(self, s, base):
                    self.s, self.base, self.n = s, base, 0

                def __call__(self, ins):
                    ins.then_inc(self.s, 1)
                    self.n += 1
                    dve.wait_ge(self.s, self.base + self.n)

            def hidden(p, k):
                n = count(p, k)
                dve.wait_ge(up_ready, n)
                if k < HALVES:
                    dve.wait_ge(silu_done, n)
                    src = g
                else:
                    dve.wait_ge(gw_done, p[2] * ROUTED + k - HALVES + 1)
                    src = gw
                wait(dve, hi_done, n - 2)
                wait(dve, lo_done, n - 2)
                v.tensor_tensor(h[:, k % 2, :], src[:, k % 3, :], up_ps[k % 3][:], ALU.mult).then_inc(h_done, 1)

            def cut_h(p, k):
                n = count(p, k)
                dve.wait_ge(hi_done, n)
                v.tensor_tensor(h_lo[:, k % HR, :], h[:, k % 2, :], h_hi[:, k % HR, :].bitcast(F32),
                                ALU.subtract).then_inc(lo_done, 1)

            def ln(l, c, src, ready, value):
                link = Links(ln_link[l], c * LN_LINKS)

                def moments():
                    dve.wait_ge(ready, value)
                    for t in range(T):
                        ins = v.bn_stats(stats[:, t, :], src[:, t, :])
                    link(ins)
                    v.memset(nt[:], 0.0)
                    for t in range(T):
                        ins = v.bn_aggr(mv[:, t, :], stats[:, t, :])
                    link(ins)
                    link(v.tensor_scalar(ve[:], mv[:, :, 1], EPS, None, ALU.add))

                def root():
                    v.tensor_scalar(vh[:], ve[:], -0.5, None, ALU.mult)
                    link(v.tensor_scalar(nt[:].bitcast(I32), ve[:].bitcast(I32), 1, None,
                                         ALU.logical_shift_right))
                    link(v.tensor_scalar(rstd[:].bitcast(I32), nt[:].bitcast(I32), -1.0, float(RSQRT_MAGIC),
                                         ALU.mult, ALU.add))

                def newton():
                    for _ in range(NEWTON):
                        link(v.tensor_tensor(nt[:], rstd[:], rstd[:], ALU.mult))
                        link(v.tensor_tensor(nt[:], nt[:], vh[:], ALU.mult))
                        link(v.scalar_tensor_tensor(out=rstd[:], in0=nt[:], scalar=1.5, in1=rstd[:],
                                                    op0=ALU.add, op1=ALU.mult))
                    assert link.n == LN_LINKS

                def normalize():
                    wait(dve, xnT_ready[l], c)
                    for t in range(T):
                        ins = v.tensor_scalar(xn[l][:, t, :], src[:, t, :], mv[:, t, 0:1], rstd[:, t:t + 1],
                                              ALU.subtract, ALU.mult)
                    ins.then_inc(xn_done[l], 1)
                return moments, root, newton, normalize

            def cut_xn(l, c, bank):
                def piece():
                    dve.wait_ge(xt_hi_done[l], c + 1)
                    v.tensor_tensor(xt_lo[l][:], bank[:], xt_hi[l][:].bitcast(F32),
                                    ALU.subtract).then_inc(xt_lo_done[l], 1)
                return piece

            def route(l, c, bank):
                link = Links(route_link[l], c * ROUTE_LINKS)
                L, neg, pos, pt = lg[l], lneg[l], lpos[l], rt[l]

                def clamp():
                    dve.wait_ge(logits_ready[l], c + 1)
                    link(v.tensor_tensor(L[:], bank[:, 0:T * E].rearrange("p (t e) -> p t e", t=T),
                                         rbias_sb[:].rearrange("p (o e) -> p o e", o=1).to_broadcast([P, T, E]),
                                         ALU.add))
                    v.tensor_scalar(neg[:], L[:], -1.0, None, ALU.min)
                    v.tensor_scalar(pos[:], L[:], -1.0, None, ALU.max).then_inc(clamped[l], 1)

                def probs():
                    dve.wait_ge(clamped[l], c + 1)
                    link(v.reciprocal(pt[:, 2], neg[:]))
                    dve.wait_ge(sig_done[l], c + 1)
                    v.tensor_tensor(pt[:, 0], pt[:, 0], pt[:, 2], ALU.mult)
                    link(v.tensor_scalar(pt[:, 1], pt[:, 1], 0.5, 0.5, ALU.mult, ALU.add))
                    v.scalar_tensor_tensor(out=pt[:, 0], in0=L[:], scalar=-1.0, in1=pt[:, 0],
                                           op0=ALU.is_lt, op1=ALU.mult)
                    link(v.scalar_tensor_tensor(out=pt[:, 1], in0=L[:], scalar=-1.0, in1=pt[:, 1],
                                                op0=ALU.is_ge, op1=ALU.mult))
                    link(v.tensor_tensor(pr[l][:], pt[:, 0], pt[:, 1], ALU.add))

                def ranks():
                    pe_ = pr[l][:].rearrange("p t (e o) -> p t e o", o=1).to_broadcast([P, T, E, E])
                    pj = pr[l][:].rearrange("p t (o j) -> p t o j", o=1).to_broadcast([P, T, E, E])
                    v.tensor_tensor(beats[:], pj, pe_, ALU.is_gt)
                    link(v.tensor_tensor(ties[:], pj, pe_, ALU.is_equal))
                    link(v.tensor_tensor(ties[:], ties[:], tri_sb[:].rearrange("p (o e) j -> p o e j", o=1)
                                         .to_broadcast([P, T, E, E]), ALU.mult))

                def count_ranks():
                    link(v.tensor_tensor(beats[:], beats[:], ties[:], ALU.add))
                    link(v.tensor_reduce(rank[:], beats[:], AX.X, ALU.add))

                def weights():
                    link(v.scalar_tensor_tensor(out=pr[l][:], in0=rank[:], scalar=1.5, in1=pr[l][:],
                                                op0=ALU.is_lt, op1=ALU.mult))
                    link(v.tensor_reduce(top[:], pr[l][:], AX.X, ALU.add))
                    link(v.reciprocal(top[:], top[:]))
                    wait(dve, wT_ready[l], c)
                    v.tensor_tensor(wtok[l][:].rearrange("p e t -> p t e"), pr[l][:], top[:].rearrange("p (t o) -> p t o", o=1)
                                    .to_broadcast([P, T, E]), ALU.mult).then_inc(wtok_done[l], 1)
                    assert link.n == ROUTE_LINKS, link.n
                return clamp, probs, ranks, count_ranks, weights

            def add_y(l, c, bank, dst, res, done, *waits):
                def piece():
                    dve.wait_ge(y_tok_ready[l], c + 1)
                    for s, n in waits:
                        wait(dve, s, n)
                    v.scalar_tensor_tensor(out=dst[:].rearrange("p t d -> p (t d)"), in0=bank[:], scalar=0.5,
                                           in1=res[:].rearrange("p t d -> p (t d)"),
                                           op0=ALU.mult, op1=ALU.add).then_inc(done, 1)
                return piece

            def q_part(c, bank, table, dst, ready, done):
                def piece():
                    dve.wait_ge(ready, c + 1)
                    wait(dve, q_rot_done, c)
                    v.tensor_tensor(dst[:], bank[:], table[:], ALU.mult).then_inc(done, 1)
                return piece

            def k_parts(c, bank):
                def piece():
                    dve.wait_ge(k_ready, c + 1)
                    wait(dve, k_rot_done, c)
                    half = DK // 2
                    for t in range(T):
                        src = bank[:, t * D:(t + 1) * D].rearrange("p (h d) -> p h d", h=NH)

                        def table(tb, a, b):
                            return tb[:, t:t + 1, a:b].to_broadcast([P, NH, b - a])
                        v.tensor_tensor(kc[:, t, :].rearrange("p (h d) -> p h d", h=NH), src,
                                        table(cost, 0, DK), ALU.mult)
                        kr = ks_[:, t, :].rearrange("p (h d) -> p h d", h=NH)
                        v.tensor_tensor(kr[:, :, 0:half], src[:, :, half:DK], table(sint, 0, half), ALU.mult)
                        ins = v.tensor_tensor(kr[:, :, half:DK], src[:, :, 0:half], table(sint, half, DK), ALU.mult)
                    ins.then_inc(k_parts_done, 1)
                return piece

            def mask_kv(c, bank):
                def piece():
                    dve.wait_ge(kv_ready, c + 1)
                    wait(dve, num_ready, c)
                    v.tensor_tensor(kv_bd[:], bank[:, 0:D], bmask[:], ALU.mult)
                    v.tensor_scalar(ks_bd[:], hmask[:], bank[:, D:D + 1], None, ALU.mult).then_inc(kv_bd_done, 1)
                return piece

            def invert(c, bank):
                def piece():
                    dve.wait_ge(den_ready, c + 1)
                    v.tensor_scalar(den[:], bank[:, 0:T * NH], float(S), None, ALU.add).then_inc(den_link, 1)
                    dve.wait_ge(den_link, c + 1)
                    wait(dve, rdenT_ready, c)
                    v.reciprocal(rden[:], den[:]).then_inc(rden_done, 1)
                return piece

            def tap(c, j):
                def piece():
                    dve.wait_ge(conv0_done, c + 1)
                    if j > 1:
                        dve.wait_ge(conv_link, 4 * c + j - 1)
                    v.scalar_tensor_tensor(out=conv[:, j % 2, :],
                                           in0=vT[:, j:j + S], scalar=taps[:, j:j + 1], in1=conv[:, (j - 1) % 2, :],
                                           op0=ALU.mult, op1=ALU.add).then_inc(conv_link, 1)
                return piece

            def attend(c, bank):
                def piece():
                    dve.wait_ge(num_ready, c + 1)
                    dve.wait_ge(rbc_done, c + 1)
                    dve.wait_ge(vT_done, c + 1)
                    wait(dve, oT_done, c)
                    v.scalar_tensor_tensor(out=att[:], in0=bank[:], scalar=vsum[:, 0:1], in1=rden_bc[:],
                                           op0=ALU.add, op1=ALU.mult).then_inc(att_done, 1)
                return piece

            def apply_gate(c):
                def piece():
                    dve.wait_ge(att_done, c + 1)
                    dve.wait_ge(conv_link, 4 * c + 4)
                    v.tensor_tensor(att[:], att[:], conv[:, 0, :], ALU.add).then_inc(o_sum_done, 1)
                    dve.wait_ge(o_sum_done, c + 1)
                    dve.wait_ge(og_done, c + 1)
                    wait(dve, proj_ready, c)
                    v.tensor_tensor(oT[:], att[:], ogate[:], ALU.mult).then_inc(oT_done, 1)
                return piece

            def add_attention(c, bank):
                def piece():
                    dve.wait_ge(proj_ready, c + 1)
                    wait(dve, x3_done, c)
                    v.tensor_tensor(x2[:].rearrange("p t d -> p (t d)"), bank[:],
                                    x1[:].rearrange("p t d -> p (t d)"), ALU.add).then_inc(x2_done, 1)
                return piece

            def phase_a(i, cur, prev, o):
                c = i - 1
                norm, r = ln(3, c, x2, x2_done, c + 1), route(3, c, misc[0])
                at = {1: (mask_kv(c, misc[0]),), 1.5: (tap(c, 1),), 2: (invert(c, misc[1]),), 3: (tap(c, 2),),
                      4: (tap(c, 3),), 5: (tap(c, 4),), 6: (attend(c, misc[0]), apply_gate(c)),
                      8: (add_attention(c, misc[0]), norm[0]), 9: norm[1:3], 10: norm[3:],
                      12: (cut_xn(3, c, misc[1]),), 13.5: r[0:1], 14.5: r[1:2], 15: r[2:3], 16: r[3:]}
                if o is not None:
                    at[7] = (add_y(3, o, misc[1], x3, x2, x3_done, (x3_free, 16 * o + 16)),)
                steps(at, cur, prev)

            def phase_b(i, cur, prev, n):
                norm = ln(2, i, x1, x1_done, i + 1)
                at = {6: (add_y(1, i, misc[1], x1, x_res, x1_done, (x_res_loaded, 16 * i + 16), (x2_done, i)),),
                      7: norm[0:2], 8: norm[2:3], 9: norm[3:], 11: (cut_xn(2, i, misc[1]),),
                      13: (q_part(i, misc[0], cosf, qc, q_ready, q_cos_done),),
                      14: (q_part(i, misc[1], sinf, qs, qp_ready, q_sin_done),),
                      15: (k_parts(i, misc[0]),)}
                if n is not None:
                    first, r = ln(1, n, x_ln, x_ln_loaded, 16 * n + 16), route(1, n, misc[0])
                    at[0], at[1], at[2], at[4] = first[0:2], first[2:3], first[3:], (cut_xn(1, n, misc[1]),)
                    at[6] += r[0:1]
                    at[10], at[12] = r[1:2], r[2:3]
                    at[13] += r[3:4]
                    at[14] += r[4:5]
                steps(at, cur, prev)

            def steps(at, cur, prev):
                for k in range(STEPS):
                    p, j = (cur, k - 1) if k else (prev, STEPS - 1)
                    if p:
                        hidden(p, j)
                    for piece in at.get(k, ()):
                        piece()
                    if p:
                        cut_h(p, j)
                    for piece in at.get(k + 0.5, ()):
                        piece()

            def cut_weights(e):
                dve.wait_ge(w_hi_done, e + 1)
                v.tensor_tensor(w_lo[:, e], raw[:, e % 3], w_hi[:, e].bitcast(F32), ALU.subtract).then_inc(w_lo_done, 1)

            for piece in ln(1, 0, x_ln, x_ln_loaded, 16):
                piece()
            dve.wait_ge(attn_hi_done, 1)
            v.tensor_tensor(aw_lo[:], raw_attn[:], aw_hi[:].bitcast(F32), ALU.subtract).then_inc(attn_lo_done, 1)
            cut_xn(1, 0, misc[1])()
            cut_weights(0)
            dve.wait_ge(ident_loaded, 48)
            first_route = route(1, 0, misc[0])
            first_route[0]()
            cut_weights(1)
            for piece in first_route[1:]:
                piece()
            for e in range(2, NE):
                cut_weights(e)
            steps({}, F1(0), None)
            dve.wait_ge(const_loaded, 160)
            dve.wait_ge(pads_set, 1)
            phase_b(0, None, F1(0), 1)
            phase_a(1, F1(1), None, None)
            with dve.Fori(1, B - 1) as i:
                phase_b(i, F2(i - 1), F1(i), i + 1)
                phase_a(i + 1, F1(i + 1), F2(i - 1), i - 1)
            phase_b(B - 1, F2(B - 2), F1(B - 1), None)
            phase_a(B, None, F2(B - 2), B - 2)
            steps({}, F2(B - 1), None)
            steps({}, None, F2(B - 1))
            add_y(3, B - 1, misc[1], x3, x2, x3_done, (x3_free, 16 * B))()

    return nc


def shape_constants():
    f = np.float32
    inv = (f(1.0) / f(10000.0) ** (np.arange(0, DK, 2, dtype=f) / f(DK))).astype(f)
    freq = np.arange(S, dtype=f)[:, None] * inv[None, :]
    emb = np.concatenate([freq, freq], axis=-1)
    cos, sin = np.cos(emb).astype(f), np.sin(emb).astype(f)
    sin[:, :DK // 2] *= f(-1.0)
    head = np.arange(D) // DK
    scale = f(DK ** -0.5)
    expand = np.zeros((T * NH, T, D), f)
    for t in range(T):
        for hd in range(NH):
            expand[t * NH + hd, t, head == hd] = 1.0
    return {
        "cos_f": np.ascontiguousarray(np.tile(cos, (1, NH)).T), "sin_f": np.ascontiguousarray(np.tile(sin, (1, NH)).T),
        "cos_t": cos, "sin_t": sin,
        "blockmask": (head[:, None] == head[None, :]).astype(f) * scale,
        "headmask": (head[:, None] == np.arange(NH)[None, :]).astype(f) * scale,
        "expand": expand,
        "tri": (np.arange(E)[None, :] < np.arange(E)[:, None]).astype(f).reshape(1, E * E),
        "ident_in": np.eye(P, dtype=f),
    }


def kernel(**inputs):
    import concourse.bacc as bacc
    from concourse.bass_utils import run_bass_kernel_spmd

    a = {n: np.asarray(v) for n, v in inputs.items()}
    wqT = a["L0_attn_Wq"].T
    arrays = {
        "x": a["L0_attn_hidden_states"],
        "wq": wqT, "wqp": wqT.reshape(D, NH, 2, DK // 2)[:, :, ::-1, :].reshape(D, D),
        "wk": a["L0_attn_Wk"].T, "wv": a["L0_attn_Wv"].T, "wg": a["L0_attn_Wg"].T, "wo": a["L0_attn_Wo"].T,
        "lepe_w": a["L0_attn_lepe_w"], "lepe_b": a["L0_attn_lepe_b"],
        "sgate": a["L0_ffn_shared_gate"].T, "sup": a["L0_ffn_shared_up"].T, "sdown": a["L0_ffn_shared_down"].T,
        "gate_w": a["L0_ffn_gate_w"], "up_w": a["L0_ffn_up_w"], "down_w": a["L0_ffn_down_w"],
        "router": a["L0_ffn_router_w"].T, "rbias": a["L0_ffn_routing_bias"],
    }
    arrays.update(shape_constants())
    nc = bacc.Bacc("TRN2", target_bir_lowering=False, num_devices=1)
    named, args = {}, {}
    for name, array in arrays.items():
        named[f"{name}_dram"] = np.ascontiguousarray(array)
        args[name] = nc.dram_tensor(f"{name}_dram", array.shape, F32, kind="ExternalInput").ap()
    args["out"] = nc.dram_tensor("out_dram", [B, S, D], F32, kind="ExternalOutput").ap()
    build(nc, **args)
    r = run_bass_kernel_spmd(nc, [named], core_ids=[0])
    return r.results[0]["out_dram"]
```

```python
from contextlib import ExitStack

import numpy as np
import concourse.bass as bass
from concourse import mybir

P = 128
ALU = mybir.AluOpType
ACT = mybir.ActivationFunctionType
AX = mybir.AxisListType
F32 = mybir.dt.float32
F32R = mybir.dt.float32r
I32 = mybir.dt.int32

B, S, D = 8, 512, 128
T = S // P
NH, DK = 8, 16
E = 8
NE = E + 1
I = 256
HALVES = I // P
STEPS = NE * HALVES
ROUTED = E * HALVES
TAPS = 5
PAD = TAPS // 2
HR = 6
WD = 4
VW = D + 2
LAG = 4
EPS = 1e-5
RSQRT_MAGIC = 0x5F3759DF
NEWTON = 3
LN_LINKS = 5 + 3 * NEWTON
ROUTE_LINKS = 12


def build(nc, x, wq, wqp, wk, wv, wg, wo, lepe_w, lepe_b, sgate, sup, sdown, gate_w, up_w, down_w,
          router, rbias, cos_f, sin_f, cos_t, sin_t, blockmask, headmask, expand, tri, ident_in, out):
    with ExitStack() as ctx:
        def sb(name, shape, dt=F32):
            return ctx.enter_context(nc.sbuf_tensor(name, shape, dt))

        def ps(name):
            return ctx.enter_context(nc.psum_tensor(name, [P, 512], F32))

        def sem(name):
            return ctx.enter_context(nc.semaphore(name))

        gate_ps = [ps(f"gate_ps{i}") for i in range(2)]
        up_ps = [ps(f"up_ps{i}") for i in range(3)]
        down_ps = ps("down_ps")
        misc = [ps(f"misc{i}") for i in range(2)]

        EW = 3 * I
        raw = sb("raw_weights", [P, 3, EW])
        w_hi = sb("w_hi", [P, NE, EW], F32R)
        w_lo = sb("w_lo", [P, NE, EW], F32R)
        NA = 5
        raw_attn = sb("raw_attn", [P, NA * D + E])
        aw_hi = sb("aw_hi", [P, NA * D + E], F32R)
        aw_lo = sb("aw_lo", [P, NA * D + E], F32R)
        Q, QP, K, V, G = [slice(i * D, (i + 1) * D) for i in range(NA)]
        R = slice(NA * D, NA * D + E)
        wo_sb = sb("wo_sb", [P, D])
        taps = sb("taps", [P, TAPS])
        tap_bias = sb("tap_bias", [P, 1])
        rbias_sb = sb("rbias_sb", [P, E])
        cosf = sb("cosf", [P, S])
        sinf = sb("sinf", [P, S])
        cost = sb("cost", [P, T, DK])
        sint = sb("sint", [P, T, DK])
        bmask = sb("bmask", [P, D])
        hmask = sb("hmask", [P, NH])
        expd = sb("expd", [T * NH, T, D])
        tri_sb = sb("tri_sb", [P, E, E])
        ident = sb("ident", [P, P])
        x_ln = sb("x_ln", [P, T, D])
        x_res = sb("x_res", [P, T, D])
        x1 = sb("x1", [P, T, D])
        x2 = sb("x2", [P, T, D])
        x3 = sb("x3", [P, T, D])
        xn = {l: sb(f"xn{l}", [P, T, D]) for l in (1, 2, 3)}
        xt_hi = {l: sb(f"xt_hi{l}", [P, S], F32R) for l in (1, 2, 3)}
        xt_lo = {l: sb(f"xt_lo{l}", [P, S], F32R) for l in (1, 2, 3)}
        stats = sb("stats", [P, T, 6])
        mv = sb("mv", [P, T, 2])
        ve = sb("ve", [P, T])
        vh = sb("vh", [P, T])
        nt = sb("nt", [P, T])
        rstd = sb("rstd", [P, T])
        lg = {l: sb(f"lg{l}", [P, T, E]) for l in (1, 3)}
        lneg = {l: sb(f"lneg{l}", [P, T, E]) for l in (1, 3)}
        lpos = {l: sb(f"lpos{l}", [P, T, E]) for l in (1, 3)}
        rt = {l: sb(f"rt{l}", [P, 3, T, E]) for l in (1, 3)}
        pr = {l: sb(f"pr{l}", [P, T, E]) for l in (1, 3)}
        beats = sb("beats", [P, T, E, E])
        ties = sb("ties", [P, T, E, E])
        rank = sb("rank", [P, T, E])
        top = sb("top", [P, T])
        wtok = {l: sb(f"wtok{l}", [P, E, T]) for l in (1, 3)}
        wT = {l: sb(f"wT{l}", [T * E, P]) for l in (1, 3)}
        w_bc = {l: sb(f"w_bc{l}", [P, E, S]) for l in (1, 3)}
        g = sb("g", [P, 3, S])
        gw = sb("gw", [P, 3, S])
        h = sb("h", [P, 2, S])
        h_hi = sb("h_hi", [P, HR, S], F32R)
        h_lo = sb("h_lo", [P, HR, S], F32R)
        yT = sb("yT", [P, S])
        qc = sb("qc", [P, S])
        qs = sb("qs", [P, S])
        q_rot = sb("q_rot", [P, S])
        k_tok = sb("k_tok", [P, T, D])
        ks_ = sb("ks", [P, T, D])
        k_rot = sb("k_rot", [P, T, D])
        v_tok = sb("v_tok", [P, T, VW])
        vT = sb("vT", [P, S + 2 * PAD])
        vsum = sb("vsum", [P, 1])
        ogate = sb("ogate", [P, S])
        kv_bd = sb("kv_bd", [P, D])
        ks_bd = sb("ks_bd", [P, NH])
        den = sb("den", [P, T * NH])
        rden = sb("rden", [P, T * NH])
        rdenT = sb("rdenT", [T * NH, P])
        rden_bc = sb("rden_bc", [P, S])
        spare = raw[:].rearrange("p r n -> p (r n)")
        conv = spare[:, 0:S]
        tapped = spare[:, S:2 * S]
        att = spare[:, 2 * S:3 * S]
        oT = spare[:, 3 * S:4 * S]

        w_dram = {l: nc.dram_tensor(f"w_scratch{l}", [B, T * E, P], F32).ap() for l in (1, 3)}

        w_loaded = [sem(f"w_loaded{i}") for i in range(3)]
        attn_loaded, const_loaded, ident_loaded = sem("attn_loaded"), sem("const_loaded"), sem("ident_loaded")
        x_ln_loaded, x_res_loaded = sem("x_ln_loaded"), sem("x_res_loaded")
        w_hi_done, w_lo_done, attn_hi_done, attn_lo_done = sem("w_hi_done"), sem("w_lo_done"), sem("attn_hi_done"), sem("attn_lo_done")
        pads_set = sem("pads_set")
        gate_ready, up_ready, silu_done, gw_done = sem("gate_ready"), sem("up_ready"), sem("silu_done"), sem("gw_done")
        h_done, hi_done, lo_done, down_done = sem("h_done"), sem("hi_done"), sem("lo_done"), sem("down_done")
        acc_copied = sem("acc_copied")
        ln_link = {l: sem(f"ln_link{l}") for l in (1, 2, 3)}
        xn_done = {l: sem(f"xn_done{l}") for l in (1, 2, 3)}
        xnT_ready = {l: sem(f"xnT_ready{l}") for l in (1, 2, 3)}
        xt_hi_done = {l: sem(f"xt_hi_done{l}") for l in (1, 2, 3)}
        xt_lo_done = {l: sem(f"xt_lo_done{l}") for l in (1, 2, 3)}
        logits_ready = {l: sem(f"logits_ready{l}") for l in (1, 3)}
        clamped = {l: sem(f"clamped{l}") for l in (1, 3)}
        sig_done = {l: sem(f"sig_done{l}") for l in (1, 3)}
        route_link = {l: sem(f"route_link{l}") for l in (1, 3)}
        wtok_done = {l: sem(f"wtok_done{l}") for l in (1, 3)}
        wT_ready = {l: sem(f"wT_ready{l}") for l in (1, 3)}
        wT_copied = {l: sem(f"wT_copied{l}") for l in (1, 3)}
        w_stored = {l: sem(f"w_stored{l}") for l in (1, 3)}
        w_bc_loaded = {l: [sem(f"w_bc_loaded{l}_{i}") for i in range(WD)] for l in (1, 3)}
        y_tok_ready = {l: sem(f"y_tok_ready{l}") for l in (1, 3)}
        x1_done, x2_done, x3_done, x3_free = sem("x1_done"), sem("x2_done"), sem("x3_done"), sem("x3_free")
        q_ready, qp_ready, k_ready, vT_ready, v_ready, og_ready = (sem(n) for n in (
            "q_ready", "qp_ready", "k_ready", "vT_ready", "v_ready", "og_ready"))
        q_cos_done, q_sin_done, q_rot_done = sem("q_cos_done"), sem("q_sin_done"), sem("q_rot_done")
        k_copied, k_link, k_rot_done = sem("k_copied"), sem("k_link"), sem("k_rot_done")
        tap_done = sem("tap_done")
        vT_done, v_tok_done, og_done = sem("vT_done"), sem("v_tok_done"), sem("og_done")
        kv_ready, kv_bd_done, den_ready, den_link = sem("kv_ready"), sem("kv_bd_done"), sem("den_ready"), sem("den_link")
        rden_done, rdenT_ready, rdenT_done, rbc_ready, rbc_done = (sem(n) for n in (
            "rden_done", "rdenT_ready", "rdenT_done", "rbc_ready", "rbc_done"))
        conv0_done, conv_link, num_ready, att_done = sem("conv0_done"), sem("conv_link"), sem("num_ready"), sem("att_done")
        o_sum_done, oT_done, proj_ready = sem("o_sum_done"), sem("oT_done"), sem("proj_ready")

        def wait(eng, s, value):
            if not isinstance(value, int) or value > 0:
                eng.wait_ge(s, value)

        def F1(c):
            return 1, c, (0 if isinstance(c, int) and c == 0 else 2 * c - 1)

        def F2(c):
            return 3, c, (2 * B - 1 if isinstance(c, int) and c == B - 1 else 2 * c + 2)

        def count(p, k):
            return p[2] * STEPS + k + 1

        def run_phase(pieces, cur, prev, front, back, back_lag):
            for k in range(STEPS):
                if cur:
                    front(cur, k)
                j = k - back_lag
                if back and j >= 0 and cur:
                    back(cur, j)
                if back and j < 0 and prev:
                    back(prev, STEPS + j)
                for piece in pieces.get(k, ()):
                    piece()

        block = ctx.enter_context(nc.Block())

        @block.sync
        def _(sp):
            def load_x_ln(c):
                wait(sp, xn_done[1], c)
                sp.dma_start(x_ln[:], x[c].rearrange("(t p) d -> p t d", p=P)).then_inc(x_ln_loaded, 16)

            def load_x_res(c):
                wait(sp, x1_done, c)
                sp.dma_start(x_res[:], x[c].rearrange("(t p) d -> p t d", p=P)).then_inc(x_res_loaded, 16)

            def spread_weights(l, c, p_before):
                wait(sp, wT_copied[l], c + 1)
                sp.dma_start(w_dram[l][c], wT[l][:]).then_inc(w_stored[l], 16)
                wait(sp, w_stored[l], 16 * c + 16)
                if p_before is not None:
                    wait(sp, gw_done, p_before[2] * ROUTED + ROUTED)
                rows = T * E // WD
                for i in range(WD):
                    sp.dma_start(w_bc[l][:, i * E // WD:(i + 1) * E // WD].rearrange("p e n -> p (e n)"),
                                 w_dram[l][c, i * rows:(i + 1) * rows].rearrange("(o r) n -> o (r n)", o=1)
                                 .to_broadcast([P, rows * P])).then_inc(w_bc_loaded[l][i], 16)

            def store(c):
                wait(sp, x3_done, c + 1)
                sp.dma_start(out[c].rearrange("(t p) d -> p t d", p=P), x3[:]).then_inc(x3_free, 16)

            sp.sem_inc(x3_free, 16)
            load_x_ln(0)
            sp.dma_start(ident[:], ident_in).then_inc(ident_loaded, 16)
            for o, w in enumerate((wq, wqp, wk, wv, wg)):
                sp.dma_start(raw_attn[:, o * D:(o + 1) * D], w).then_inc(attn_loaded, 16)
            sp.dma_start(raw_attn[:, R], router).then_inc(attn_loaded, 16)
            sp.dma_start(rbias_sb[:], rbias.rearrange("(o e) -> o e", o=1).to_broadcast([P, E])).then_inc(ident_loaded, 16)
            sp.dma_start(tri_sb[:].rearrange("p e j -> p (e j)"), tri.to_broadcast([P, E * E])).then_inc(ident_loaded, 16)
            for e in range(NE):
                wait(sp, w_lo_done, e - 2)
                r = raw[:, e % 3]
                gs, us, ds = (sgate, sup, sdown) if e == 0 else (gate_w[e - 1], up_w[e - 1], down_w[e - 1])
                sp.dma_start(r[:, 0:I], gs).then_inc(w_loaded[e % 3], 16)
                sp.dma_start(r[:, I:2 * I], us).then_inc(w_loaded[e % 3], 16)
                sp.dma_start(r[:, 2 * I:].rearrange("p (s d) -> p s d", s=HALVES),
                             ds.rearrange("(s p) d -> p s d", p=P)).then_inc(w_loaded[e % 3], 16)
                if e == 1:
                    for dst, src in ((wo_sb[:], wo), (taps[:], lepe_w.rearrange("d o k -> d (o k)")),
                                     (tap_bias[:], lepe_b.rearrange("(d o) -> d o", o=1)),
                                     (cosf[:], cos_f), (sinf[:], sin_f),
                                     (cost[:], cos_t.rearrange("(t p) d -> p t d", p=P)),
                                     (sint[:], sin_t.rearrange("(t p) d -> p t d", p=P)),
                                     (bmask[:], blockmask), (hmask[:], headmask), (expd[:], expand)):
                        sp.dma_start(dst, src).then_inc(const_loaded, 16)
                if e == 2:
                    spread_weights(1, 0, None)
            load_x_res(0)
            load_x_ln(1)
            spread_weights(1, 1, F1(0))
            load_x_res(1)
            load_x_ln(2)
            spread_weights(3, 0, None)

            def middle(i, last):
                spread_weights(1, i + 1, F1(i))
                load_x_res(i + 1)
                if not last:
                    load_x_ln(i + 2)
                store(i - 1)
                spread_weights(3, i, F2(i - 1))
            with sp.Fori(1, B - 2) as i:
                middle(i, False)
            middle(B - 2, True)
            store(B - 2)
            spread_weights(3, B - 1, F2(B - 2))
            store(B - 1)
            sp.wait_ge(x3_free, 16 * B + 16)

        @block.tensor
        def _(pe):
            def product3(dst, w_h, w_l, m_h, m_l, start, stop):
                pe.matmul(dst, w_h, m_h, start=start, stop=False)
                pe.matmul(dst, w_l, m_h, start=False, stop=False)
                return pe.matmul(dst, w_h, m_l, start=False, stop=stop)

            def gate_up(p, k):
                l, c, _ = p
                n, e, half = count(p, k), k // HALVES, k % HALVES
                if k == 0:
                    pe.wait_ge(xt_lo_done[l], c + 1)
                if isinstance(p[2], int) and p[2] == 0 and half == 0:
                    pe.wait_ge(w_lo_done, e + 1)
                wait(pe, silu_done, n - 2)
                at = slice(half * P, half * P + P)
                product3(gate_ps[k % 2][:], w_hi[:, e, at], w_lo[:, e, at], xt_hi[l][:], xt_lo[l][:],
                         True, True).then_inc(gate_ready, 1)
                wait(pe, h_done, n - 3)
                at = slice(I + half * P, I + half * P + P)
                product3(up_ps[k % 3][:], w_hi[:, e, at], w_lo[:, e, at], xt_hi[l][:], xt_lo[l][:],
                         True, True).then_inc(up_ready, 1)

            def down(p, k):
                n, e, half = count(p, k), k // HALVES, k % HALVES
                pe.wait_ge(lo_done, n)
                if k == 0:
                    wait(pe, acc_copied, p[2])
                at = slice(2 * I + half * D, 2 * I + half * D + D)
                product3(down_ps[:], w_hi[:, e, at], w_lo[:, e, at], h_hi[:, k % HR, :], h_lo[:, k % HR, :],
                         k == 0, k == STEPS - 1).then_inc(down_done, 1)

            def turn(l, src, ready, value, bank, free, done):
                def piece():
                    pe.wait_ge(ready, value)
                    for s, v in free:
                        wait(pe, s, v)
                    for t in range(T):
                        mm = pe.transpose(bank[:, t * P:(t + 1) * P], src(t), ident[:])
                    mm.then_inc(done, 1)
                return piece

            def xn_turn(l, c, bank, *free):
                return turn(l, lambda t: xn[l][:, t, :], xn_done[l], c + 1, bank, free, xnT_ready[l])

            def y_turn(l, p, bank, *free):
                return turn(l, lambda t: yT[:, t * P:(t + 1) * P], acc_copied, p[2] + 1, bank, free,
                            y_tok_ready[l])

            def logits(l, c, bank, *free):
                def piece():
                    pe.wait_ge(xt_lo_done[l], c + 1)
                    for s, v in free:
                        wait(pe, s, v)
                    for t in range(T):
                        tile = slice(t * P, (t + 1) * P)
                        mm = product3(bank[:, t * E:(t + 1) * E], xt_hi[l][:, tile], xt_lo[l][:, tile],
                                      aw_hi[:, R], aw_lo[:, R], True, True)
                    mm.then_inc(logits_ready[l], 1)
                return piece

            def w_turn(l, c, bank, *free):
                def piece():
                    pe.wait_ge(wtok_done[l], c + 1)
                    for s, v in free:
                        wait(pe, s, v)
                    pe.transpose(bank[0:T * E, 0:P], wtok[l][:].rearrange("p e t -> p (e t)"),
                                 ident[:]).then_inc(wT_ready[l], 1)
                return piece

            def project(c, w, bank, done, *free):
                def piece():
                    pe.wait_ge(xt_lo_done[2], c + 1)
                    for s, v in free:
                        wait(pe, s, v)
                    product3(bank[:], aw_hi[:, w], aw_lo[:, w], xt_hi[2][:], xt_lo[2][:],
                             True, True).then_inc(done, 1)
                return piece

            def project_tokens(c, w, bank, done, *free):
                def piece():
                    pe.wait_ge(xt_lo_done[2], c + 1)
                    for s, v in free:
                        wait(pe, s, v)
                    for t in range(T):
                        tile = slice(t * P, (t + 1) * P)
                        mm = product3(bank[:, t * D:(t + 1) * D], xt_hi[2][:, tile], xt_lo[2][:, tile],
                                      aw_hi[:, w], aw_lo[:, w], True, True)
                    mm.then_inc(done, 1)
                return piece

            def kv(c, bank, *free):
                def piece():
                    pe.wait_ge(k_rot_done, c + 1)
                    pe.wait_ge(v_tok_done, c + 1)
                    for s, v in free:
                        wait(pe, s, v)
                    for t in range(T):
                        mm = pe.matmul(bank[:, 0:VW], k_rot[:, t, :], v_tok[:, t, :], start=t == 0, stop=t == T - 1)
                    mm.then_inc(kv_ready, 1)
                return piece

            def denominators(c, bank, *free):
                def piece():
                    pe.wait_ge(kv_bd_done, c + 1)
                    pe.wait_ge(q_rot_done, c + 1)
                    for s, v in free:
                        wait(pe, s, v)
                    for t in range(T):
                        mm = pe.matmul(bank[:, t * NH:(t + 1) * NH], q_rot[:, t * P:(t + 1) * P], ks_bd[:],
                                       start=True, stop=True)
                    mm.then_inc(den_ready, 1)
                return piece

            def rden_turn(c, bank, *free):
                def piece():
                    pe.wait_ge(rden_done, c + 1)
                    for s, v in free:
                        wait(pe, s, v)
                    pe.transpose(bank[0:T * NH, 0:P], rden[:], ident[:]).then_inc(rdenT_ready, 1)
                return piece

            def rden_spread(c, bank, *free):
                def piece():
                    pe.wait_ge(rdenT_done, c + 1)
                    for s, v in free:
                        wait(pe, s, v)
                    for t in range(T):
                        mm = pe.matmul(bank[:, t * P:(t + 1) * P], expd[:, t, :], rdenT[:], start=True, stop=True)
                    mm.then_inc(rbc_ready, 1)
                return piece

            def numerators(c, bank, *free):
                def piece():
                    pe.wait_ge(kv_bd_done, c + 1)
                    pe.wait_ge(q_rot_done, c + 1)
                    for s, v in free:
                        wait(pe, s, v)
                    pe.matmul(bank[:], kv_bd[:], q_rot[:], start=True, stop=True).then_inc(num_ready, 1)
                return piece

            def out_project(c, bank, *free):
                def piece():
                    pe.wait_ge(oT_done, c + 1)
                    for s, v in free:
                        wait(pe, s, v)
                    for t in range(T):
                        mm = pe.matmul(bank[:, t * D:(t + 1) * D], oT[:, t * P:(t + 1) * P], wo_sb[:],
                                       start=True, stop=True)
                    mm.then_inc(proj_ready, 1)
                return piece

            m0, m1 = misc

            def prep1(n, a):
                return (xn_turn(1, n, m1, (x1_done, n)),
                        logits(1, n, m0, (clamped[3], a + 1)),
                        w_turn(1, n, m1, (og_done, n)))

            def attn1(c, prev1, prev0, *before_xn2):
                return (y_turn(1, F1(c), m1, prev1),
                        xn_turn(2, c, m1, (x1_done, c + 1), *before_xn2),
                        project_tokens(c, K, m0, k_ready, prev0),
                        project(c, Q, m0, q_ready, (k_copied, c + 1)),
                        project(c, QP, m1, qp_ready, (xt_lo_done[2], c + 1)),
                        project(c, V, m1, vT_ready, (q_sin_done, c + 1)),
                        project_tokens(c, V, m0, v_ready, (q_cos_done, c + 1)),
                        project(c, G, m1, og_ready, (vT_done, c + 1)))

            def attn2(c, *before_den):
                return (kv(c, m0, (v_tok_done, c + 1)),
                        denominators(c, m1, (og_done, c + 1), *before_den),
                        rden_turn(c, m0, (kv_bd_done, c + 1)),
                        rden_spread(c, m1, (den_link, c + 1)),
                        numerators(c, m0, (rdenT_done, c + 1)),
                        out_project(c, m0, (att_done, c + 1)),
                        xn_turn(3, c, m1, (rbc_done, c + 1), (x3_done, c)),
                        logits(3, c, m0, (x2_done, c + 1)),
                        )

            def phase_a(i, cur, prev, o):
                a = attn2(i - 1)
                at = {1: a[2:3], 2: a[3:5], 6: a[5:6], 10: a[6:7], 11: a[7:8], 17: (w_turn(3, i - 1, m1, (xt_lo_done[3], i)),)}
                if o is not None:
                    at[5] = (y_turn(3, F2(o), m1, (rbc_done, i)),)
                run_phase(at, cur, prev, gate_up, down, LAG)

            def phase_b(i, cur, prev, n):
                prev1 = (wT_copied[3], i)
                prev0 = (clamped[1], i + 2) if n is not None else (clamped[3], i)
                c = attn1(i, prev1, prev0, *(((xt_lo_done[1], i + 2),) if n is not None else ()))
                a = attn2(i, *(((wT_copied[1], i + 2),) if n is not None else ()))
                at = {4: c[0:1], 8: c[1:2], 9: c[2:3], 10: c[3:4], 11: c[4:5], 12: c[5:6], 13: c[6:7], 14: c[7:8],
                      15: a[0:1], 17: a[1:2]}
                if n is not None:
                    r = prep1(n, i - 1)
                    at[5], at[7], at[16] = r[0:1], r[1:2], r[2:3]
                run_phase(at, cur, prev, gate_up, down, LAG)

            pe.wait_ge(ident_loaded, 48)
            xn_turn(1, 0, m1)()
            pe.wait_ge(attn_lo_done, 1)
            logits(1, 0, m0)()
            w_turn(1, 0, m1)()
            run_phase({}, F1(0), None, gate_up, down, LAG)
            pe.wait_ge(const_loaded, 160)
            phase_b(0, None, F1(0), 1)
            phase_a(1, F1(1), None, None)
            with pe.Fori(1, B - 1) as i:
                phase_b(i, F2(i - 1), F1(i), i + 1)
                phase_a(i + 1, F1(i + 1), F2(i - 1), i - 1)
            phase_b(B - 1, F2(B - 2), F1(B - 1), None)
            phase_a(B, None, F2(B - 2), B - 2)
            run_phase({}, F2(B - 1), None, gate_up, down, LAG)
            run_phase({}, None, F2(B - 1), gate_up, down, LAG)
            y_turn(3, F2(B - 1), m1, (wT_copied[3], B))()

        @block.scalar
        def _(act):
            def silu(p, k):
                n = count(p, k)
                act.wait_ge(gate_ready, n)
                wait(act, h_done, n - 3)
                nc.scalar.activation(g[:, k % 3, :], gate_ps[k % 2][:], ACT.Silu).then_inc(silu_done, 1)

            def round_h(p, k):
                n = count(p, k)
                act.wait_ge(h_done, n)
                wait(act, down_done, n - HR)
                nc.scalar.activation(h_hi[:, k % HR, :], h[:, k % 2, :], ACT.Copy).then_inc(hi_done, 1)

            def copy(dst, src, ready, value, done, *free):
                def piece():
                    act.wait_ge(ready, value)
                    for s, v in free:
                        wait(act, s, v)
                    nc.scalar.activation(dst, src, ACT.Copy).then_inc(done, 1)
                return piece

            def copy_out(p, l):
                return copy(yT[:], down_ps[:], down_done, p[2] * STEPS + STEPS, acc_copied)

            def round_xn(l, c, bank, *free):
                return copy(xt_hi[l][:], bank[:], xnT_ready[l], c + 1, xt_hi_done[l], *free)

            def sigmoids(l, c):
                def piece():
                    act.wait_ge(clamped[l], c + 1)
                    nc.scalar.activation(rt[l][:, 0], lneg[l][:], ACT.Silu)
                    nc.scalar.activation(rt[l][:, 1], lpos[l][:], ACT.Tanh, scale=0.5).then_inc(sig_done[l], 1)
                return piece

            def copy_wT(l, c, bank):
                return copy(wT[l][:], bank[0:T * E, 0:P], wT_ready[l], c + 1, wT_copied[l],
                            (w_stored[l], 16 * c))

            def values_T(c):
                def piece():
                    act.wait_ge(vT_ready, c + 1)
                    wait(act, conv_link, 4 * c)
                    wait(act, att_done, c)
                    nc.scalar.activation(vT[:, PAD:PAD + S], misc[1][:], ACT.Copy,
                                         accum_out=vsum[:]).then_inc(vT_done, 1)
                return piece

            def values_tok(c):
                return copy(v_tok[:, :, 0:D], misc[0][:].rearrange("p (t d) -> p t d", t=T), v_ready, c + 1,
                            v_tok_done, (kv_ready, c))

            def first_tap(c):
                def piece():
                    act.wait_ge(vT_done, c + 1)
                    wait(act, o_sum_done, c)
                    nc.scalar.activation(conv, vT[:, 0:S], ACT.Identity, bias=tap_bias[:, 0:1],
                                         scale=taps[:, 0:1]).then_inc(conv0_done, 1)
                return piece

            def tap(c, j):
                def piece():
                    if j > 1:
                        act.wait_ge(conv_link, 4 * c + j - 1)
                    nc.scalar.activation(tapped, vT[:, j:j + S], ACT.Copy, scale=taps[:, j:j + 1]
                                         ).then_inc(tap_done, 1)
                return piece

            def phase_a(i, cur, prev, o):
                c = i - 1
                at = {0: (tap(c, 4),), 1: (copy(rdenT[:], misc[0][0:T * NH, 0:P], rdenT_ready, c + 1, rdenT_done),),
                      3: (copy(rden_bc[:], misc[1][:], rbc_ready, c + 1, rbc_done),),
                      10: (round_xn(3, c, misc[1]),), 12: (sigmoids(3, c),), 17: (copy_wT(3, c, misc[1]),)}
                if o is not None:
                    at[3] += (copy_out(F2(o), 3),)
                run_phase(at, cur, prev, silu, round_h, 1)

            def phase_b(i, cur, prev, n):
                at = {3: (copy_out(F1(i), 1),), 8: (round_xn(2, i, misc[1]),),
                      9: (copy(k_tok[:].rearrange("p t d -> p (t d)"), misc[0][:], k_ready, i + 1, k_copied,
                                (k_link, 2 * i)),),
                      12: (values_T(i),), 13: (values_tok(i), first_tap(i)),
                      14: (copy(ogate[:], misc[1][:], og_ready, i + 1, og_done, (oT_done, i)),),
                      15: (tap(i, 1),), 16: (tap(i, 2),), 17: (tap(i, 3),)}
                if n is not None:
                    at[5] = (round_xn(1, n, misc[1]),)
                    at[9] += (sigmoids(1, n),)
                    at[16] = (copy_wT(1, n, misc[1]),) + at[16]
                run_phase(at, cur, prev, silu, round_h, 1)

            def cut_weights(e):
                act.wait_ge(w_loaded[e % 3], 48 * (e // 3 + 1))
                nc.scalar.activation(w_hi[:, e], raw[:, e % 3], ACT.Copy).then_inc(w_hi_done, 1)

            act.wait_ge(attn_loaded, 96)
            nc.scalar.activation(aw_hi[:], raw_attn[:], ACT.Copy).then_inc(attn_hi_done, 1)
            round_xn(1, 0, misc[1])()
            cut_weights(0)
            cut_weights(1)
            sigmoids(1, 0)()
            cut_weights(2)
            copy_wT(1, 0, misc[1])()
            for e in range(3, NE):
                cut_weights(e)
            run_phase({}, F1(0), None, silu, round_h, 1)
            act.wait_ge(const_loaded, 160)
            phase_b(0, None, F1(0), 1)
            phase_a(1, F1(1), None, None)
            with act.Fori(1, B - 1) as i:
                phase_b(i, F2(i - 1), F1(i), i + 1)
                phase_a(i + 1, F1(i + 1), F2(i - 1), i - 1)
            phase_b(B - 1, F2(B - 2), F1(B - 1), None)
            phase_a(B, None, F2(B - 2), B - 2)
            run_phase({}, F2(B - 1), None, silu, round_h, 1)
            run_phase({}, None, F2(B - 1), silu, round_h, 1)
            copy_out(F2(B - 1), 3)()

        @block.gpsimd
        def _(pool):
            def weigh(p, k):
                l, c, before = p
                n, e = count(p, k), k // HALVES - 1
                if e < 0:
                    return
                if k % HALVES == 0 and e % (E // WD) == 0:
                    pool.wait_ge(w_bc_loaded[l][e * WD // E], 16 * c + 16)
                pool.wait_ge(silu_done, n)
                wait(pool, h_done, n - 3)
                nc.gpsimd.tensor_tensor(gw[:, k % 3, :], g[:, k % 3, :], w_bc[l][:, e, :], ALU.mult).then_inc(gw_done, 1)

            def add_q(c):
                def piece():
                    pool.wait_ge(q_cos_done, c + 1)
                    pool.wait_ge(q_sin_done, c + 1)
                    wait(pool, num_ready, c)
                    nc.gpsimd.tensor_tensor(q_rot[:], qc[:], qs[:], ALU.add).then_inc(q_rot_done, 1)
                return piece

            def turn_k(c):
                half = DK // 2

                def heads(ap, a, b):
                    return ap[:].rearrange("p t (h d) -> p t h d", h=NH)[:, :, :, a:b]

                def table(ap, a, b):
                    return ap[:].rearrange("p t (o d) -> p t o d", o=1)[:, :, :, a:b].to_broadcast([P, T, NH, b - a])

                def cos_part():
                    pool.wait_ge(k_copied, c + 1)
                    wait(pool, kv_ready, c)
                    nc.gpsimd.tensor_tensor(heads(k_rot, 0, DK), heads(k_tok, 0, DK), table(cost, 0, DK), ALU.mult)

                def sin_part():
                    nc.gpsimd.tensor_tensor(heads(ks_, 0, half), heads(k_tok, half, DK), table(sint, 0, half),
                                            ALU.mult).then_inc(k_link, 1)
                    nc.gpsimd.tensor_tensor(heads(ks_, half, DK), heads(k_tok, 0, half), table(sint, half, DK),
                                            ALU.mult).then_inc(k_link, 1)

                def add_parts():
                    pool.wait_ge(k_link, 2 * c + 2)
                    nc.gpsimd.tensor_tensor(k_rot[:], k_rot[:], ks_[:], ALU.add).then_inc(k_rot_done, 1)
                return cos_part, sin_part, add_parts

            def add_tap(c, j):
                def piece():
                    if j == 1:
                        pool.wait_ge(conv0_done, c + 1)
                    pool.wait_ge(tap_done, 4 * c + j)
                    if j > 1:
                        pool.wait_ge(conv_link, 4 * c + j - 1)
                    nc.gpsimd.tensor_tensor(conv, conv, tapped, ALU.add).then_inc(conv_link, 1)
                return piece

            def phase_a(i, cur, prev, o):
                run_phase({0: (add_tap(i - 1, 3),), 1: (add_tap(i - 1, 4),)}, cur, prev, weigh, None, 0)

            def phase_b(i, cur, prev, n):
                k = turn_k(i)
                run_phase({10: k[0:1], 11: k[1:2], 12: k[2:3], 14: (add_q(i),), 15: (add_tap(i, 1),), 17: (add_tap(i, 2),)},
                          cur, prev, weigh, None, 0)

            nc.gpsimd.memset(vT[:], 0.0)
            nc.gpsimd.memset(v_tok[:], 1.0).then_inc(pads_set, 1)
            run_phase({}, F1(0), None, weigh, None, 0)
            phase_b(0, None, F1(0), 1)
            phase_a(1, F1(1), None, None)
            with pool.Fori(1, B - 1) as i:
                phase_b(i, F2(i - 1), F1(i), i + 1)
                phase_a(i + 1, F1(i + 1), F2(i - 1), i - 1)
            phase_b(B - 1, F2(B - 2), F1(B - 1), None)
            phase_a(B, None, F2(B - 2), B - 2)
            run_phase({}, F2(B - 1), None, weigh, None, 0)

        @block.vector
        def _(dve):
            v = nc.vector

            def chain(s, base):
                made = []

                def link(issue):
                    n = len(made)

                    def piece():
                        if n:
                            dve.wait_ge(s, base + n)
                        issue().then_inc(s, 1)
                    made.append(piece)
                    return piece
                link.made = made
                return link

            def hidden(p, k):
                n = count(p, k)
                dve.wait_ge(up_ready, n)
                if k < HALVES:
                    dve.wait_ge(silu_done, n)
                    src = g
                else:
                    dve.wait_ge(gw_done, p[2] * ROUTED + k - HALVES + 1)
                    src = gw
                wait(dve, hi_done, n - 2)
                wait(dve, lo_done, n - 2)
                v.tensor_tensor(h[:, k % 2, :], src[:, k % 3, :], up_ps[k % 3][:], ALU.mult).then_inc(h_done, 1)

            def cut_h(p, k):
                n = count(p, k)
                dve.wait_ge(hi_done, n)
                v.tensor_tensor(h_lo[:, k % HR, :], h[:, k % 2, :], h_hi[:, k % HR, :].bitcast(F32),
                                ALU.subtract).then_inc(lo_done, 1)

            def ln(l, c, src, ready, value):
                link = chain(ln_link[l], c * LN_LINKS)

                def partial():
                    dve.wait_ge(ready, value)
                    for t in range(T):
                        ins = v.bn_stats(stats[:, t, :], src[:, t, :])
                    return ins

                def aggregate():
                    v.memset(nt[:], 0.0)
                    for t in range(T):
                        ins = v.bn_aggr(mv[:, t, :], stats[:, t, :])
                    return ins

                def exponent():
                    v.tensor_scalar(vh[:], ve[:], -0.5, None, ALU.mult)
                    return v.tensor_scalar(nt[:].bitcast(I32), ve[:].bitcast(I32), 1, None,
                                           ALU.logical_shift_right)

                moments = (link(partial), link(aggregate),
                           link(lambda: v.tensor_scalar(ve[:], mv[:, :, 1], EPS, None, ALU.add)))
                root = (link(exponent),
                        link(lambda: v.tensor_scalar(rstd[:].bitcast(I32), nt[:].bitcast(I32), -1.0,
                                                     float(RSQRT_MAGIC), ALU.mult, ALU.add)))
                newton = ()
                for _ in range(NEWTON):
                    newton += (link(lambda: v.tensor_tensor(nt[:], rstd[:], rstd[:], ALU.mult)),
                               link(lambda: v.tensor_tensor(nt[:], nt[:], vh[:], ALU.mult)),
                               link(lambda: v.scalar_tensor_tensor(out=rstd[:], in0=nt[:], scalar=1.5, in1=rstd[:],
                                                                   op0=ALU.add, op1=ALU.mult)))
                assert len(link.made) == LN_LINKS

                def normalize():
                    dve.wait_ge(ln_link[l], (c + 1) * LN_LINKS)
                    wait(dve, xnT_ready[l], c)
                    for t in range(T):
                        ins = v.tensor_scalar(xn[l][:, t, :], src[:, t, :], mv[:, t, 0:1], rstd[:, t:t + 1],
                                              ALU.subtract, ALU.mult)
                    ins.then_inc(xn_done[l], 1)
                return moments, root + newton, (normalize,)

            def cut_xn(l, c, bank):
                def piece():
                    dve.wait_ge(xt_hi_done[l], c + 1)
                    v.tensor_tensor(xt_lo[l][:], bank[:], xt_hi[l][:].bitcast(F32),
                                    ALU.subtract).then_inc(xt_lo_done[l], 1)
                return piece

            def route(l, c, bank):
                link = chain(route_link[l], c * ROUTE_LINKS)
                L, neg, pos, pt = lg[l], lneg[l], lpos[l], rt[l]
                mine = pr[l][:].rearrange("p t (e o) -> p t e o", o=1).to_broadcast([P, T, E, E])
                others = pr[l][:].rearrange("p t (o j) -> p t o j", o=1).to_broadcast([P, T, E, E])
                lower = tri_sb[:].rearrange("p (o e) j -> p o e j", o=1).to_broadcast([P, T, E, E])

                def biased():
                    dve.wait_ge(logits_ready[l], c + 1)
                    return v.tensor_tensor(L[:], bank[:, 0:T * E].rearrange("p (t e) -> p t e", t=T),
                                           rbias_sb[:].rearrange("p (o e) -> p o e", o=1).to_broadcast([P, T, E]),
                                           ALU.add)

                def clamp():
                    dve.wait_ge(route_link[l], c * ROUTE_LINKS + 1)
                    v.tensor_scalar(neg[:], L[:], -1.0, None, ALU.min)
                    v.tensor_scalar(pos[:], L[:], -1.0, None, ALU.max).then_inc(clamped[l], 1)

                def inverse():
                    dve.wait_ge(clamped[l], c + 1)
                    return v.reciprocal(pt[:, 2], neg[:])

                def branches():
                    dve.wait_ge(sig_done[l], c + 1)
                    v.tensor_tensor(pt[:, 0], pt[:, 0], pt[:, 2], ALU.mult)
                    return v.tensor_scalar(pt[:, 1], pt[:, 1], 0.5, 0.5, ALU.mult, ALU.add)

                def chosen():
                    v.scalar_tensor_tensor(out=pt[:, 0], in0=L[:], scalar=-1.0, in1=pt[:, 0],
                                           op0=ALU.is_lt, op1=ALU.mult)
                    return v.scalar_tensor_tensor(out=pt[:, 1], in0=L[:], scalar=-1.0, in1=pt[:, 1],
                                                  op0=ALU.is_ge, op1=ALU.mult)

                def compare():
                    v.tensor_tensor(beats[:], others, mine, ALU.is_gt)
                    return v.tensor_tensor(ties[:], others, mine, ALU.is_equal)

                first = (link(biased), clamp)
                probs = (link(inverse), link(branches), link(chosen),
                         link(lambda: v.tensor_tensor(pr[l][:], pt[:, 0], pt[:, 1], ALU.add)))
                ranks = (link(compare),
                         link(lambda: v.tensor_tensor(ties[:], ties[:], lower, ALU.mult)),
                         link(lambda: v.tensor_tensor(beats[:], beats[:], ties[:], ALU.add)),
                         link(lambda: v.tensor_reduce(rank[:], beats[:], AX.X, ALU.add)))
                top2 = (link(lambda: v.scalar_tensor_tensor(out=pr[l][:], in0=rank[:], scalar=1.5, in1=pr[l][:],
                                                            op0=ALU.is_lt, op1=ALU.mult)),
                        link(lambda: v.tensor_reduce(top[:], pr[l][:], AX.X, ALU.add)),
                        link(lambda: v.reciprocal(top[:], top[:])))
                assert len(link.made) == ROUTE_LINKS, len(link.made)

                def weights():
                    dve.wait_ge(route_link[l], (c + 1) * ROUTE_LINKS)
                    wait(dve, wT_ready[l], c)
                    v.tensor_tensor(wtok[l][:].rearrange("p e t -> p t e"), pr[l][:],
                                    top[:].rearrange("p (t o) -> p t o", o=1).to_broadcast([P, T, E]),
                                    ALU.mult).then_inc(wtok_done[l], 1)
                return first, probs, ranks, top2 + (weights,)

            def add_y(l, c, bank, dst, res, done, *waits):
                def piece():
                    dve.wait_ge(y_tok_ready[l], c + 1)
                    for s, n in waits:
                        wait(dve, s, n)
                    v.scalar_tensor_tensor(out=dst[:].rearrange("p t d -> p (t d)"), in0=bank[:], scalar=0.5,
                                           in1=res[:].rearrange("p t d -> p (t d)"),
                                           op0=ALU.mult, op1=ALU.add).then_inc(done, 1)
                return piece

            def q_part(c, bank, table, dst, ready, done):
                def piece():
                    dve.wait_ge(ready, c + 1)
                    wait(dve, q_rot_done, c)
                    v.tensor_tensor(dst[:], bank[:], table[:], ALU.mult).then_inc(done, 1)
                return piece

            def mask_kv(c, bank):
                def piece():
                    dve.wait_ge(kv_ready, c + 1)
                    wait(dve, num_ready, c)
                    v.tensor_tensor(kv_bd[:], bank[:, 0:D], bmask[:], ALU.mult)
                    v.tensor_scalar(ks_bd[:], hmask[:], bank[:, D:D + 1], None, ALU.mult).then_inc(kv_bd_done, 1)
                return piece

            def invert(c, bank):
                def piece():
                    dve.wait_ge(den_ready, c + 1)
                    v.tensor_scalar(den[:], bank[:, 0:T * NH], float(S), None, ALU.add).then_inc(den_link, 1)
                    dve.wait_ge(den_link, c + 1)
                    wait(dve, rdenT_ready, c)
                    v.reciprocal(rden[:], den[:]).then_inc(rden_done, 1)
                return piece

            def attend(c, bank):
                def piece():
                    dve.wait_ge(num_ready, c + 1)
                    dve.wait_ge(rbc_done, c + 1)
                    dve.wait_ge(vT_done, c + 1)
                    wait(dve, oT_done, c)
                    v.scalar_tensor_tensor(out=att, in0=bank[:], scalar=vsum[:, 0:1], in1=rden_bc[:],
                                           op0=ALU.add, op1=ALU.mult).then_inc(att_done, 1)
                return piece

            def apply_gate(c):
                def piece():
                    dve.wait_ge(att_done, c + 1)
                    dve.wait_ge(conv_link, 4 * c + 4)
                    v.tensor_tensor(att, att, conv, ALU.add).then_inc(o_sum_done, 1)
                    dve.wait_ge(o_sum_done, c + 1)
                    dve.wait_ge(og_done, c + 1)
                    wait(dve, proj_ready, c)
                    v.tensor_tensor(oT, att, ogate[:], ALU.mult).then_inc(oT_done, 1)
                return piece

            def add_attention(c, bank):
                def piece():
                    dve.wait_ge(proj_ready, c + 1)
                    wait(dve, x3_done, c)
                    v.tensor_tensor(x2[:].rearrange("p t d -> p (t d)"), bank[:],
                                    x1[:].rearrange("p t d -> p (t d)"), ALU.add).then_inc(x2_done, 1)
                return piece

            def phase_a(i, cur, prev, o):
                c = i - 1
                (m, n, norm), r = ln(3, c, x2, x2_done, c + 1), route(3, c, misc[0])
                at = {0: (invert(c, misc[1]),), 4: (attend(c, misc[0]),), 5: (apply_gate(c),),
                      7: (add_attention(c, misc[0]),), 7.5: m, 8: n[0:4], 8.5: n[4:6], 9: n[6:9], 9.5: n[9:] + norm,
                      11: (cut_xn(3, c, misc[1]),), 12: r[0], 13: r[1][0:2], 13.5: r[1][2:], 14: r[2][0:2],
                      14.5: r[2][2:], 15: r[3]}
                if o is not None:
                    at[6] = (add_y(3, o, misc[1], x3, x2, x3_done, (x3_free, 16 * o + 16)),)
                steps(at, cur, prev)

            def phase_b(i, cur, prev, n):
                m, newton, norm = ln(2, i, x1, x1_done, i + 1)
                at = {5: (add_y(1, i, misc[1], x1, x_res, x1_done, (x_res_loaded, 16 * i + 16), (x2_done, i)),),
                      5.5: m, 6: newton[0:3], 6.5: newton[3:6], 7: newton[6:9], 7.5: newton[9:] + norm,
                      9: (cut_xn(2, i, misc[1]),),
                      12: (q_part(i, misc[0], cosf, qc, q_ready, q_cos_done),),
                      12.5: (q_part(i, misc[1], sinf, qs, qp_ready, q_sin_done),),
                      16.5: (mask_kv(i, misc[0]),)}
                if n is not None:
                    (m, newton, norm), r = ln(1, n, x_ln, x_ln_loaded, 16 * n + 16), route(1, n, misc[0])
                    at[0.5], at[1], at[1.5] = m, newton[0:2], newton[2:5]
                    at[2], at[2.5], at[3], at[3.5] = newton[5:7], newton[7:9], newton[9:], norm
                    at[6] = (cut_xn(1, n, misc[1]),) + at[6]
                    at[8.5] = r[0]
                    at[10], at[10.5], at[11], at[11.5], at[13] = r[1][0:2], r[1][2:], r[2][0:2], r[2][2:], r[3]
                steps(at, cur, prev)

            def steps(at, cur, prev):
                for k in range(STEPS):
                    for work, j, slot in ((hidden, k - 1, k), (cut_h, k - 2, k + 0.5)):
                        if j >= 0 and cur:
                            work(cur, j)
                        if j < 0 and prev:
                            work(prev, STEPS + j)
                        for piece in at.get(slot, ()):
                            piece()

            def cut_weights(e):
                dve.wait_ge(w_hi_done, e + 1)
                v.tensor_tensor(w_lo[:, e], raw[:, e % 3], w_hi[:, e].bitcast(F32), ALU.subtract).then_inc(w_lo_done, 1)

            for part in ln(1, 0, x_ln, x_ln_loaded, 16):
                for piece in part:
                    piece()
            dve.wait_ge(attn_hi_done, 1)
            v.tensor_tensor(aw_lo[:], raw_attn[:], aw_hi[:].bitcast(F32), ALU.subtract).then_inc(attn_lo_done, 1)
            cut_xn(1, 0, misc[1])()
            cut_weights(0)
            dve.wait_ge(ident_loaded, 48)
            first_route = route(1, 0, misc[0])
            for piece in first_route[0]:
                piece()
            cut_weights(1)
            for part in first_route[1:]:
                for piece in part:
                    piece()
            for e in range(2, NE):
                cut_weights(e)
            steps({}, F1(0), None)
            dve.wait_ge(const_loaded, 160)
            dve.wait_ge(pads_set, 1)
            phase_b(0, None, F1(0), 1)
            phase_a(1, F1(1), None, None)
            with dve.Fori(1, B - 1) as i:
                phase_b(i, F2(i - 1), F1(i), i + 1)
                phase_a(i + 1, F1(i + 1), F2(i - 1), i - 1)
            phase_b(B - 1, F2(B - 2), F1(B - 1), None)
            phase_a(B, None, F2(B - 2), B - 2)
            steps({}, F2(B - 1), None)
            steps({}, None, F2(B - 1))
            add_y(3, B - 1, misc[1], x3, x2, x3_done, (x3_free, 16 * B))()

    return nc


def shape_constants():
    f = np.float32
    inv = (f(1.0) / f(10000.0) ** (np.arange(0, DK, 2, dtype=f) / f(DK))).astype(f)
    freq = np.arange(S, dtype=f)[:, None] * inv[None, :]
    emb = np.concatenate([freq, freq], axis=-1)
    cos, sin = np.cos(emb).astype(f), np.sin(emb).astype(f)
    sin[:, :DK // 2] *= f(-1.0)
    head = np.arange(D) // DK
    scale = f(DK ** -0.5)
    expand = np.zeros((T * NH, T, D), f)
    for t in range(T):
        for hd in range(NH):
            expand[t * NH + hd, t, head == hd] = 1.0
    return {
        "cos_f": np.ascontiguousarray(np.tile(cos, (1, NH)).T), "sin_f": np.ascontiguousarray(np.tile(sin, (1, NH)).T),
        "cos_t": cos, "sin_t": sin,
        "blockmask": (head[:, None] == head[None, :]).astype(f) * scale,
        "headmask": (head[:, None] == np.arange(NH)[None, :]).astype(f) * scale,
        "expand": expand,
        "tri": (np.arange(E)[None, :] < np.arange(E)[:, None]).astype(f).reshape(1, E * E),
        "ident_in": np.eye(P, dtype=f),
    }


def kernel(**inputs):
    import concourse.bacc as bacc
    from concourse.bass_utils import run_bass_kernel_spmd

    a = {n: np.asarray(v) for n, v in inputs.items()}
    wqT = a["L0_attn_Wq"].T
    arrays = {
        "x": a["L0_attn_hidden_states"],
        "wq": wqT, "wqp": wqT.reshape(D, NH, 2, DK // 2)[:, :, ::-1, :].reshape(D, D),
        "wk": a["L0_attn_Wk"].T, "wv": a["L0_attn_Wv"].T, "wg": a["L0_attn_Wg"].T, "wo": a["L0_attn_Wo"].T,
        "lepe_w": a["L0_attn_lepe_w"], "lepe_b": a["L0_attn_lepe_b"],
        "sgate": a["L0_ffn_shared_gate"].T, "sup": a["L0_ffn_shared_up"].T, "sdown": a["L0_ffn_shared_down"].T,
        "gate_w": a["L0_ffn_gate_w"], "up_w": a["L0_ffn_up_w"], "down_w": a["L0_ffn_down_w"],
        "router": a["L0_ffn_router_w"].T, "rbias": a["L0_ffn_routing_bias"],
    }
    arrays.update(shape_constants())
    nc = bacc.Bacc("TRN2", target_bir_lowering=False, num_devices=1)
    named, args = {}, {}
    for name, array in arrays.items():
        named[f"{name}_dram"] = np.ascontiguousarray(array)
        args[name] = nc.dram_tensor(f"{name}_dram", array.shape, F32, kind="ExternalInput").ap()
    args["out"] = nc.dram_tensor("out_dram", [B, S, D], F32, kind="ExternalOutput").ap()
    build(nc, **args)
    r = run_bass_kernel_spmd(nc, [named], core_ids=[0])
    return r.results[0]["out_dram"]
```

```python
from contextlib import ExitStack

import numpy as np
import concourse.bass as bass
from concourse import mybir

P = 128
ALU = mybir.AluOpType
ACT = mybir.ActivationFunctionType
AX = mybir.AxisListType
F32 = mybir.dt.float32
F32R = mybir.dt.float32r
I32 = mybir.dt.int32

B, S, D = 8, 512, 128
T = S // P
NH, DK = 8, 16
E = 8
NE = E + 1
I = 256
HALVES = I // P
STEPS = NE * HALVES
ROUTED = E * HALVES
TAPS = 5
PAD = TAPS // 2
HR = 6
WD = 4
VW = D + 2
LAG = 4
EPS = 1e-5
RSQRT_MAGIC = 0x5F3759DF
NEWTON = 3
BY_DVE = 4
LN_LINKS = 5 + 3 * NEWTON
ROUTE_LINKS = 13


def build(nc, x, wq, wqp, wk, wv, wg, wo, lepe_w, lepe_b, sgate, sup, sdown, gate_w, up_w, down_w,
          router, rbias, cos_f, sin_f, cos_t, sin_t, blockmask, headmask, expand, tri, ident_in, out):
    with ExitStack() as ctx:
        def sb(name, shape, dt=F32):
            return ctx.enter_context(nc.sbuf_tensor(name, shape, dt))

        def ps(name):
            return ctx.enter_context(nc.psum_tensor(name, [P, 512], F32))

        def sem(name):
            return ctx.enter_context(nc.semaphore(name))

        gate_ps = [ps(f"gate_ps{i}") for i in range(2)]
        up_ps = [ps(f"up_ps{i}") for i in range(3)]
        down_ps = ps("down_ps")
        misc = [ps(f"misc{i}") for i in range(2)]

        EW = 3 * I
        raw = sb("raw_weights", [P, E // 2, EW])
        w_hi = sb("w_hi", [P, NE, EW], F32R)
        w_lo = sb("w_lo", [P, NE, EW], F32R)
        NA = 5
        raw_attn = sb("raw_attn", [P, NA * D + E])
        aw_hi = sb("aw_hi", [P, NA * D], F32R)
        aw_lo = sb("aw_lo", [P, NA * D], F32R)
        router_cut = sb("router_cut", [P, 2, E], F32R)
        Q, QP, K, V, G = [slice(i * D, (i + 1) * D) for i in range(NA)]
        R = slice(NA * D, NA * D + E)
        wo_sb = sb("wo_sb", [P, D])
        taps = sb("taps", [P, TAPS])
        tap_bias = sb("tap_bias", [P, 1])
        rbias_sb = sb("rbias_sb", [P, E])
        cosf = sb("cosf", [P, S])
        sinf = sb("sinf", [P, S])
        cost = sb("cost", [P, T, DK])
        sint = sb("sint", [P, T, DK])
        bmask = sb("bmask", [P, D])
        hmask = sb("hmask", [P, NH])
        expd = sb("expd", [T * NH, T, D])
        tri_sb = sb("tri_sb", [P, E, E])
        ident = sb("ident", [P, P])
        x_ln = sb("x_ln", [P, T, D])
        x_res = sb("x_res", [P, T, D])
        x1 = sb("x1", [P, T, D])
        x2 = sb("x2", [P, T, D])
        x3 = sb("x3", [P, T, D])
        xn = {l: sb(f"xn{l}", [P, T, D]) for l in (1, 2, 3)}
        xt_hi = {l: sb(f"xt_hi{l}", [P, S], F32R) for l in (1, 2, 3)}
        xt_lo = {l: sb(f"xt_lo{l}", [P, S], F32R) for l in (1, 2, 3)}
        stats = sb("stats", [P, T, 6])
        mv = sb("mv", [P, T, 2])
        ve = sb("ve", [P, T])
        vh = sb("vh", [P, T])
        nt = sb("nt", [P, T])
        rstd = sb("rstd", [P, T])
        lg = {l: sb(f"lg{l}", [P, T, E]) for l in (1, 3)}
        lneg = {l: sb(f"lneg{l}", [P, T, E]) for l in (1, 3)}
        lpos = {l: sb(f"lpos{l}", [P, T, E]) for l in (1, 3)}
        rt = {l: sb(f"rt{l}", [P, 3, T, E]) for l in (1, 3)}
        pr = {l: sb(f"pr{l}", [P, T, E]) for l in (1, 3)}
        beats = sb("beats", [P, T, E, E])
        ties = sb("ties", [P, T, E, E])
        rank = sb("rank", [P, T, E])
        top = sb("top", [P, T])
        wtok = {l: sb(f"wtok{l}", [P, E, T]) for l in (1, 3)}
        wT = {l: sb(f"wT{l}", [T * E, P]) for l in (1, 3)}
        w_bc = {l: sb(f"w_bc{l}", [P, E, S]) for l in (1, 3)}
        g = sb("g", [P, 3, S])
        gw = sb("gw", [P, 3, S])
        h = sb("h", [P, 2, S])
        h_hi = sb("h_hi", [P, HR, S], F32R)
        h_lo = sb("h_lo", [P, HR, S], F32R)
        yT = sb("yT", [P, S])
        qc = sb("qc", [P, S])
        qs = sb("qs", [P, S])
        q_rot = sb("q_rot", [P, S])
        k_rot = sb("k_rot", [P, T, D])
        v_tok = sb("v_tok", [P, T, VW])
        vT = sb("vT", [P, S + 2 * PAD])
        vsum = sb("vsum", [P, 1])
        ogate = sb("ogate", [P, S])
        kv_bd = sb("kv_bd", [P, D])
        ks_bd = sb("ks_bd", [P, NH])
        den = sb("den", [P, T * NH])
        rden = sb("rden", [P, T * NH])
        rdenT = sb("rdenT", [T * NH, P])
        rden_bc = sb("rden_bc", [P, S])
        spare = raw[:].rearrange("p r n -> p (r n)")
        conv, att, oT, k_tok, ks_ = [spare[:, n * S:(n + 1) * S] for n in range(5)]
        k_tok, ks_ = [ap.rearrange("p (t d) -> p t d", t=T) for ap in (k_tok, ks_)]
        early = w_bc[1][:].rearrange("p e n -> p (e n)")[:, 0:(1 + E // 2) * EW].rearrange("p (r n) -> p r n", n=EW)

        def uncut(e, n=1):
            if e == 0:
                return early[:, E // 2:]
            e -= 1
            return early[:, e:e + n] if e < E // 2 else raw[:, e - E // 2:e - E // 2 + n]

        w_dram = {l: nc.dram_tensor(f"w_scratch{l}", [B, T * E, P], F32).ap() for l in (1, 3)}

        w_loaded = [sem(f"w_loaded{i}") for i in range(1 + E // 2)]
        router_loaded, router_hi_done, router_lo_done = sem("router_loaded"), sem("router_hi_done"), sem("router_lo_done")
        attn_loaded, const_loaded, ident_loaded = sem("attn_loaded"), sem("const_loaded"), sem("ident_loaded")
        x_ln_loaded, x_res_loaded = sem("x_ln_loaded"), sem("x_res_loaded")
        w_lo_pool_done = sem("w_lo_pool_done")
        w_hi_done, w_lo_done, attn_hi_done, attn_lo_done = sem("w_hi_done"), sem("w_lo_done"), sem("attn_hi_done"), sem("attn_lo_done")
        pads_set = sem("pads_set")
        gate_ready, up_ready, silu_done, gw_done = sem("gate_ready"), sem("up_ready"), sem("silu_done"), sem("gw_done")
        h_done, hi_done, lo_done, down_done = sem("h_done"), sem("hi_done"), sem("lo_done"), sem("down_done")
        acc_copied = sem("acc_copied")
        ln_link = {l: sem(f"ln_link{l}") for l in (1, 2, 3)}
        xn_done = {l: sem(f"xn_done{l}") for l in (1, 2, 3)}
        xnT_ready = {l: sem(f"xnT_ready{l}") for l in (1, 2, 3)}
        xt_hi_done = {l: sem(f"xt_hi_done{l}") for l in (1, 2, 3)}
        xt_lo_done = {l: sem(f"xt_lo_done{l}") for l in (1, 2, 3)}
        logits_ready = {l: sem(f"logits_ready{l}") for l in (1, 3)}
        clamped = {l: sem(f"clamped{l}") for l in (1, 3)}
        sig_done = {l: sem(f"sig_done{l}") for l in (1, 3)}
        route_link = {l: sem(f"route_link{l}") for l in (1, 3)}
        wtok_done = {l: sem(f"wtok_done{l}") for l in (1, 3)}
        wT_ready = {l: sem(f"wT_ready{l}") for l in (1, 3)}
        wT_copied = {l: sem(f"wT_copied{l}") for l in (1, 3)}
        w_stored = {l: sem(f"w_stored{l}") for l in (1, 3)}
        w_bc_loaded = {l: [sem(f"w_bc_loaded{l}_{i}") for i in range(WD)] for l in (1, 3)}
        y_tok_ready = {l: sem(f"y_tok_ready{l}") for l in (1, 3)}
        x1_done, x2_done, x3_done, x3_free = sem("x1_done"), sem("x2_done"), sem("x3_done"), sem("x3_free")
        q_ready, qp_ready, k_ready, vT_ready, v_ready, og_ready = (sem(n) for n in (
            "q_ready", "qp_ready", "k_ready", "vT_ready", "v_ready", "og_ready"))
        q_cos_done, q_sin_done, q_rot_done = sem("q_cos_done"), sem("q_sin_done"), sem("q_rot_done")
        k_copied, k_link, k_rot_done = sem("k_copied"), sem("k_link"), sem("k_rot_done")
        vT_done, v_tok_done, og_done = sem("vT_done"), sem("v_tok_done"), sem("og_done")
        kv_ready, kv_bd_done, den_ready, den_link = sem("kv_ready"), sem("kv_bd_done"), sem("den_ready"), sem("den_link")
        rden_done, rdenT_ready, rdenT_done, rbc_ready, rbc_done = (sem(n) for n in (
            "rden_done", "rdenT_ready", "rdenT_done", "rbc_ready", "rbc_done"))
        conv0_done, conv_link, num_ready, att_done = sem("conv0_done"), sem("conv_link"), sem("num_ready"), sem("att_done")
        o_sum_done, oT_done, proj_ready = sem("o_sum_done"), sem("oT_done"), sem("proj_ready")

        def wait(eng, s, value):
            if not isinstance(value, int) or value > 0:
                eng.wait_ge(s, value)

        def F1(c):
            return 1, c, (0 if isinstance(c, int) and c == 0 else 2 * c - 1)

        def F2(c):
            return 3, c, (2 * B - 1 if isinstance(c, int) and c == B - 1 else 2 * c + 2)

        def count(p, k):
            return p[2] * STEPS + k + 1

        def side(l, c):
            if isinstance(c, int) and (l, c) in ((1, 0), (3, B - 1)):
                return 4 - l
            return l

        def every(p):
            return [(p, k) for k in range(STEPS)]

        def spaced(p, first, slots):
            work = [None] * STEPS
            for n, slot in enumerate(slots):
                work[slot] = (p, first + n)
            return work

        def last(p, end=STEPS):
            return [(p, k) for k in range(end - LAG, end)]

        WIDE = ((0, 1, 2, 3, 6, 7, 9, 10, 13, 15, 17),
                (2, 4, 7, 10, 11, 15, 17))
        FIRST = len(WIDE[0])
        assert FIRST + len(WIDE[1]) == STEPS

        def place(*items):
            at = {}
            for slot, pieces in items:
                at.setdefault(slot, []).extend(pieces if isinstance(pieces, tuple) else (pieces,))
            return at

        def run_phase(pieces, work, before, front, back, back_lag):
            steps = before + [step for step in work if step]
            n = len(before)
            for k in range(STEPS):
                if work[k]:
                    front(*work[k])
                for piece in pieces.get(k - 0.5, ()):
                    piece()
                if work[k]:
                    if back and n >= back_lag:
                        back(*steps[n - back_lag])
                    n += 1
                for piece in pieces.get(k, ()):
                    piece()

        block = ctx.enter_context(nc.Block())

        aw_raw = raw_attn[:, 0:NA * D]
        router_raw = raw_attn[:, R]

        @block.sync
        def _(sp):
            def load_x_ln(c):
                wait(sp, xn_done[1], c)
                sp.dma_start(x_ln[:], x[c].rearrange("(t p) d -> p t d", p=P)).then_inc(x_ln_loaded, 16)

            def load_x_res(c):
                wait(sp, x1_done, c)
                sp.dma_start(x_res[:], x[c].rearrange("(t p) d -> p t d", p=P)).then_inc(x_res_loaded, 16)

            def spread_weights(l, c, p_before):
                wait(sp, wT_copied[l], c + 1)
                sp.dma_start(w_dram[l][c], wT[l][:]).then_inc(w_stored[l], 16)
                wait(sp, w_stored[l], 16 * c + 16)
                if p_before is not None:
                    wait(sp, gw_done, p_before[2] * ROUTED + ROUTED)
                rows = T * E // WD
                for i in range(WD):
                    sp.dma_start(w_bc[side(l, c)][:, i * E // WD:(i + 1) * E // WD].rearrange("p e n -> p (e n)"),
                                 w_dram[l][c, i * rows:(i + 1) * rows].rearrange("(o r) n -> o (r n)", o=1)
                                 .to_broadcast([P, rows * P])).then_inc(w_bc_loaded[l][i], 16)

            def store(c):
                wait(sp, x3_done, c + 1)
                sp.dma_start(out[c].rearrange("(t p) d -> p t d", p=P), x3[:]).then_inc(x3_free, 16)

            sp.sem_inc(x3_free, 16)
            load_x_ln(0)
            sp.dma_start(router_raw, router).then_inc(router_loaded, 16)
            sp.dma_start(ident[:], ident_in).then_inc(ident_loaded, 16)

            def load_weights(n, experts, gs, us, ds):
                dst = uncut(experts.start, experts.stop - experts.start)
                sp.dma_start(dst[:, :, 0:I], gs).then_inc(w_loaded[n], 16)
                sp.dma_start(dst[:, :, I:2 * I], us).then_inc(w_loaded[n], 16)
                for j in range(experts.stop - experts.start):
                    sp.dma_start(dst[:, j, 2 * I:].rearrange("p (s d) -> p s d", s=HALVES),
                                 ds[j].rearrange("(s p) d -> p s d", p=P)).then_inc(w_loaded[n], 16)

            load_weights(0, slice(0, 1), sgate.rearrange("p (e n) -> p e n", e=1),
                         sup.rearrange("p (e n) -> p e n", e=1), (sdown,))
            sp.dma_start(rbias_sb[:], rbias.rearrange("(o e) -> o e", o=1).to_broadcast([P, E])).then_inc(ident_loaded, 16)
            sp.dma_start(tri_sb[:].rearrange("p e j -> p (e j)"), tri.to_broadcast([P, E * E])).then_inc(ident_loaded, 16)
            for n in range(E // 2):
                pair = slice(2 * n, 2 * n + 2)
                load_weights(n + 1, slice(2 * n + 1, 2 * n + 3), gate_w[pair].rearrange("e p n -> p e n"),
                             up_w[pair].rearrange("e p n -> p e n"), (down_w[2 * n], down_w[2 * n + 1]))
            load_x_ln(1)
            for o, w in enumerate((wq, wqp, wk, wv, wg)):
                sp.dma_start(aw_raw[:, o * D:(o + 1) * D], w).then_inc(attn_loaded, 16)
            spread_weights(1, 0, None)
            load_x_res(0)
            for dst, src in ((wo_sb[:], wo), (taps[:], lepe_w.rearrange("d o k -> d (o k)")),
                             (tap_bias[:], lepe_b.rearrange("(d o) -> d o", o=1)),
                             (cosf[:], cos_f), (sinf[:], sin_f),
                             (cost[:], cos_t.rearrange("(t p) d -> p t d", p=P)),
                             (sint[:], sin_t.rearrange("(t p) d -> p t d", p=P)),
                             (bmask[:], blockmask), (hmask[:], headmask), (expd[:], expand)):
                sp.dma_start(dst, src).then_inc(const_loaded, 16)
            sp.wait_ge(w_lo_done, BY_DVE)
            sp.wait_ge(w_lo_pool_done, NE - BY_DVE)
            spread_weights(1, 1, None)
            load_x_res(1)
            load_x_ln(2)
            spread_weights(3, 0, F1(0))

            def middle(i, last):
                if not last:
                    load_x_ln(i + 2)
                spread_weights(1, i + 1, F1(i))
                load_x_res(i + 1)
                store(i - 1)
                spread_weights(3, i, F2(i - 1))
            with sp.Fori(1, B - 2) as i:
                middle(i, False)
            middle(B - 2, True)
            spread_weights(3, B - 1, F1(B - 1))
            store(B - 2)
            store(B - 1)
            sp.wait_ge(x3_free, 16 * B + 16)

        @block.tensor
        def _(pe):
            def product3(dst, w_h, w_l, m_h, m_l, start, stop):
                pe.matmul(dst, w_h, m_h, start=start, stop=False)
                pe.matmul(dst, w_l, m_h, start=False, stop=False)
                return pe.matmul(dst, w_h, m_l, start=False, stop=stop)

            def gate_up(p, k):
                l, c, _ = p
                m_hi, m_lo = xt_hi[side(l, c)], xt_lo[side(l, c)]
                n, e, half = count(p, k), k // HALVES, k % HALVES
                if k == 0:
                    pe.wait_ge(xt_lo_done[l], c + 1)
                if isinstance(p[2], int) and p[2] == 0 and half == 0:
                    pe.wait_ge(w_lo_done, min(e + 1, BY_DVE))
                    if e >= BY_DVE:
                        pe.wait_ge(w_lo_pool_done, e + 1 - BY_DVE)
                wait(pe, silu_done, n - 2)
                at = slice(half * P, half * P + P)
                product3(gate_ps[k % 2][:], w_hi[:, e, at], w_lo[:, e, at], m_hi[:], m_lo[:],
                         True, True).then_inc(gate_ready, 1)
                wait(pe, h_done, n - 3)
                at = slice(I + half * P, I + half * P + P)
                product3(up_ps[k % 3][:], w_hi[:, e, at], w_lo[:, e, at], m_hi[:], m_lo[:],
                         True, True).then_inc(up_ready, 1)

            def down(p, k):
                n, e, half = count(p, k), k // HALVES, k % HALVES
                pe.wait_ge(lo_done, n)
                if k == 0:
                    wait(pe, acc_copied, p[2])
                at = slice(2 * I + half * D, 2 * I + half * D + D)
                product3(down_ps[:], w_hi[:, e, at], w_lo[:, e, at], h_hi[:, k % HR, :], h_lo[:, k % HR, :],
                         k == 0, k == STEPS - 1).then_inc(down_done, 1)

            def turn(src, ready, value, bank, free, done):
                def piece():
                    pe.wait_ge(ready, value)
                    for s, v in free:
                        wait(pe, s, v)
                    for t in range(T):
                        mm = pe.transpose(bank[:, t * P:(t + 1) * P], src(t), ident[:])
                    mm.then_inc(done, 1)
                return piece

            def xn_turn(l, c, bank, *free):
                return turn(lambda t: xn[l][:, t, :], xn_done[l], c + 1, bank, free, xnT_ready[l])

            def y_turn(l, p, bank, *free):
                return turn(lambda t: yT[:, t * P:(t + 1) * P], acc_copied, p[2] + 1, bank, free, y_tok_ready[l])

            def logits(l, c, bank, *free):
                def piece():
                    pe.wait_ge(xt_lo_done[l], c + 1)
                    for s, v in free:
                        wait(pe, s, v)
                    for t in range(T):
                        tile = slice(t * P, (t + 1) * P)
                        pe.matmul(bank[:, 2 * t * E:2 * (t + 1) * E], xt_hi[side(l, c)][:, tile],
                                  router_cut[:].rearrange("p r e -> p (r e)"), start=True, stop=False)
                        mm = pe.matmul(bank[:, 2 * t * E:(2 * t + 1) * E], xt_lo[side(l, c)][:, tile],
                                       router_cut[:, 0], start=False, stop=True)
                    mm.then_inc(logits_ready[l], 1)
                return piece

            def w_turn(l, c, bank, *free):
                def piece():
                    pe.wait_ge(wtok_done[l], c + 1)
                    for s, v in free:
                        wait(pe, s, v)
                    pe.transpose(bank[0:T * E, 0:P], wtok[l][:].rearrange("p e t -> p (e t)"),
                                 ident[:]).then_inc(wT_ready[l], 1)
                return piece

            def project(c, w, bank, done, *free):
                def piece():
                    pe.wait_ge(xt_lo_done[2], c + 1)
                    for s, v in free:
                        wait(pe, s, v)
                    product3(bank[:], aw_hi[:, w], aw_lo[:, w], xt_hi[2][:], xt_lo[2][:],
                             True, True).then_inc(done, 1)
                return piece

            def project_tokens(c, w, bank, done, *free):
                def piece():
                    pe.wait_ge(xt_lo_done[2], c + 1)
                    for s, v in free:
                        wait(pe, s, v)
                    for t in range(T):
                        tile = slice(t * P, (t + 1) * P)
                        mm = product3(bank[:, t * D:(t + 1) * D], xt_hi[2][:, tile], xt_lo[2][:, tile],
                                      aw_hi[:, w], aw_lo[:, w], True, True)
                    mm.then_inc(done, 1)
                return piece

            def kv(c, bank, *free):
                def piece():
                    pe.wait_ge(k_rot_done, c + 1)
                    pe.wait_ge(v_tok_done, c + 1)
                    for s, v in free:
                        wait(pe, s, v)
                    for t in range(T):
                        mm = pe.matmul(bank[:, 0:VW], k_rot[:, t, :], v_tok[:, t, :], start=t == 0, stop=t == T - 1)
                    mm.then_inc(kv_ready, 1)
                return piece

            def denominators(c, bank, *free):
                def piece():
                    pe.wait_ge(kv_bd_done, c + 1)
                    pe.wait_ge(q_rot_done, c + 1)
                    for s, v in free:
                        wait(pe, s, v)
                    for t in range(T):
                        mm = pe.matmul(bank[:, t * NH:(t + 1) * NH], q_rot[:, t * P:(t + 1) * P], ks_bd[:],
                                       start=True, stop=True)
                    mm.then_inc(den_ready, 1)
                return piece

            def rden_turn(c, bank, *free):
                def piece():
                    pe.wait_ge(rden_done, c + 1)
                    for s, v in free:
                        wait(pe, s, v)
                    pe.transpose(bank[0:T * NH, 0:P], rden[:], ident[:]).then_inc(rdenT_ready, 1)
                return piece

            def rden_spread(c, bank, *free):
                def piece():
                    pe.wait_ge(rdenT_done, c + 1)
                    for s, v in free:
                        wait(pe, s, v)
                    for t in range(T):
                        mm = pe.matmul(bank[:, t * P:(t + 1) * P], expd[:, t, :], rdenT[:], start=True, stop=True)
                    mm.then_inc(rbc_ready, 1)
                return piece

            def numerators(c, bank, *free):
                def piece():
                    pe.wait_ge(kv_bd_done, c + 1)
                    pe.wait_ge(q_rot_done, c + 1)
                    for s, v in free:
                        wait(pe, s, v)
                    pe.matmul(bank[:], kv_bd[:], q_rot[:], start=True, stop=True).then_inc(num_ready, 1)
                return piece

            def out_project(c, bank, *free):
                def piece():
                    pe.wait_ge(oT_done, c + 1)
                    for s, v in free:
                        wait(pe, s, v)
                    for t in range(T):
                        mm = pe.matmul(bank[:, t * D:(t + 1) * D], oT[:, t * P:(t + 1) * P], wo_sb[:],
                                       start=True, stop=True)
                    mm.then_inc(proj_ready, 1)
                return piece

            m0, m1 = misc

            def prep1(n, a):
                return (xn_turn(1, n, m1, (wT_copied[3], a + 1)),
                        logits(1, n, m0, (clamped[3], a + 1)),
                        w_turn(1, n, m1, (og_done, n)))

            def attn1(c, prev1, prev0):
                return (y_turn(1, F1(c), m1, prev1),
                        xn_turn(2, c, m1, (x1_done, c + 1)),
                        project_tokens(c, K, m0, k_ready, prev0),
                        project(c, Q, m0, q_ready, (k_copied, c + 1)),
                        project(c, QP, m1, qp_ready, (xt_lo_done[2], c + 1)),
                        project(c, V, m1, vT_ready, (q_sin_done, c + 1)),
                        turn(lambda t: vT[:, PAD + t * P:PAD + (t + 1) * P], vT_done, c + 1, m0,
                             ((q_cos_done, c + 1),), v_ready),
                        project(c, G, m1, og_ready, (vT_done, c + 1)))

            def attn2(c, *before_den):
                return (kv(c, m0, (v_tok_done, c + 1)),
                        denominators(c, m1, (og_done, c + 1), *before_den),
                        rden_turn(c, m0, (kv_bd_done, c + 1)),
                        rden_spread(c, m1, (den_link, c + 1)),
                        numerators(c, m0, (rdenT_done, c + 1)),
                        out_project(c, m0, (att_done, c + 1)),
                        xn_turn(3, c, m1, (rbc_done, c + 1), *(((x3_done, c),) if side(3, c) == 3 else ())),
                        logits(3, c, m0, (x2_done, c + 1)),
                        )

            def phase_a(i, work, before, o):
                w = None in work
                a = attn2(i - 1)
                at = [((0.5, 0)[w], a[2]), ((2, 2)[w], a[3]), ((2, 3)[w], a[4]), ((4.5, 3.5)[w], a[5]), ((9.5, 10)[w], a[6]),
                      ((10.5, 10.5)[w], a[7]), ((17, 17)[w], w_turn(3, i - 1, m1, (xt_lo_done[3], i)))]
                if o is not None:
                    at.append(((4, 5)[w], y_turn(3, F2(o), m1, (rbc_done, i))))
                run_phase(place(*at), work, before, gate_up, down, LAG)

            def phase_b(i, work, before, n):
                w = None in work
                if isinstance(i, int) and i == 0:
                    free1, free0 = (wT_copied[1], 2), (clamped[1], 2)
                else:
                    free1 = (wT_copied[3], i) if n is None else (xt_lo_done[1], i + 2)
                    free0 = (clamped[3], i) if n is None else (clamped[1], i + 2)
                c = attn1(i, free1, free0)
                a = attn2(i, *(((wT_copied[1], i + 2),) if n is not None else ()))
                at = [((4, 3.5)[w], c[0]), ((7.5, 8.5)[w], c[1]), ((8.5, 9.5)[w], c[2]), ((10, 11)[w], c[3]), ((11, 11)[w], c[4]),
                      ((12, 12.5)[w], c[5]), ((12.5, 13.5)[w], c[6]), ((13, 14)[w], c[7]), ((14, 16.5)[w], a[0]), ((16, 17)[w], a[1])]
                if n is not None:
                    r = prep1(n, i - 1)
                    at += [((1.5, 4.5)[w], r[0]), ((3.5, 7)[w], r[1]), ((15.5, 17)[w], r[2])]
                run_phase(place(*at), work, before, gate_up, down, LAG)

            pe.wait_ge(ident_loaded, 48)
            xn_turn(1, 0, m1)()
            pe.wait_ge(router_lo_done, 1)
            logits(1, 0, m0)()
            run_phase(place((1, w_turn(1, 0, m1)), (4, xn_turn(1, 1, m1, (wT_copied[1], 1))),
                            (6.5, logits(1, 1, m0, (clamped[1], 1))), (14.5, w_turn(1, 1, m1, (xt_lo_done[1], 2)))),
                      every(F1(0)), [], gate_up, down, LAG)
            pe.wait_ge(const_loaded, 160)
            pe.wait_ge(attn_lo_done, 1)
            phase_b(0, spaced(F1(1), 0, WIDE[0]), last(F1(0)), None)
            phase_a(1, spaced(F1(1), FIRST, WIDE[1]), last(F1(1), FIRST), None)
            with pe.Fori(1, B - 1) as i:
                phase_b(i, every(F2(i - 1)), last(F1(i)), i + 1)
                phase_a(i + 1, every(F1(i + 1)), last(F2(i - 1)), i - 1)
            phase_b(B - 1, spaced(F2(B - 2), 0, WIDE[0]), last(F1(B - 1)), None)
            phase_a(B, spaced(F2(B - 2), FIRST, WIDE[1]), last(F2(B - 2), FIRST), None)
            run_phase(place((5, y_turn(3, F2(B - 2), m1, (wT_copied[3], B)))), every(F2(B - 1)), last(F2(B - 2)),
                      gate_up, down, LAG)
            for step in last(F2(B - 1)):
                down(*step)
            y_turn(3, F2(B - 1), m1, (x3_done, B - 1))()

        @block.scalar
        def _(act):
            def silu(p, k):
                n = count(p, k)
                act.wait_ge(gate_ready, n)
                wait(act, h_done, n - 3)
                nc.scalar.activation(g[:, k % 3, :], gate_ps[k % 2][:], ACT.Silu).then_inc(silu_done, 1)

            def round_h(p, k):
                n = count(p, k)
                act.wait_ge(h_done, n)
                wait(act, down_done, n - HR)
                nc.scalar.activation(h_hi[:, k % HR, :], h[:, k % 2, :], ACT.Copy).then_inc(hi_done, 1)

            def copy(dst, src, ready, value, done, *free):
                def piece():
                    act.wait_ge(ready, value)
                    for s, v in free:
                        wait(act, s, v)
                    nc.scalar.activation(dst, src, ACT.Copy).then_inc(done, 1)
                return piece

            def copy_out(p, l):
                return copy(yT[:], down_ps[:], down_done, p[2] * STEPS + STEPS, acc_copied)

            def round_xn(l, c, bank, *free):
                return copy(xt_hi[side(l, c)][:], bank[:], xnT_ready[l], c + 1, xt_hi_done[l], *free)

            def sigmoids(l, c):
                def piece():
                    act.wait_ge(clamped[l], c + 1)
                    nc.scalar.activation(rt[l][:, 0], lneg[l][:], ACT.Silu)
                    nc.scalar.activation(rt[l][:, 1], lpos[l][:], ACT.Tanh, scale=0.5).then_inc(sig_done[l], 1)
                return piece

            def copy_wT(l, c, bank):
                return copy(wT[l][:], bank[0:T * E, 0:P], wT_ready[l], c + 1, wT_copied[l],
                            (w_stored[l], 16 * c))

            def values_T(c):
                def piece():
                    act.wait_ge(vT_ready, c + 1)
                    wait(act, conv_link, 4 * c)
                    wait(act, att_done, c)
                    nc.scalar.activation(vT[:, PAD:PAD + S], misc[1][:], ACT.Copy,
                                         accum_out=vsum[:]).then_inc(vT_done, 1)
                return piece

            def values_tok(c):
                return copy(v_tok[:, :, 0:D], misc[0][:].rearrange("p (t d) -> p t d", t=T), v_ready, c + 1,
                            v_tok_done, (kv_ready, c))

            def first_tap(c):
                def piece():
                    act.wait_ge(vT_done, c + 1)
                    wait(act, o_sum_done, c)
                    nc.scalar.activation(conv, vT[:, 0:S], ACT.Identity, bias=tap_bias[:, 0:1],
                                         scale=taps[:, 0:1]).then_inc(conv0_done, 1)
                return piece

            def phase_a(i, work, before, o):
                w = None in work
                c = i - 1
                at = [((0.5, 1)[w], copy(rdenT[:], misc[0][0:T * NH, 0:P], rdenT_ready, c + 1, rdenT_done)),
                      ((3, 3)[w], copy(rden_bc[:], misc[1][:], rbc_ready, c + 1, rbc_done)),
                      ((8.5, 9.5)[w], round_xn(3, c, misc[1])), ((11.5, 13)[w], sigmoids(3, c)), ((15.5, 16)[w], copy_wT(3, c, misc[1]))]
                if o is not None:
                    at.append(((3, 3)[w], copy_out(F2(o), 3)))
                run_phase(place(*at), work, before[-1:], silu, round_h, 1)

            def phase_b(i, work, before, n):
                w = None in work
                at = [((2.5, 2.5)[w], copy_out(F1(i), 1)), ((7.5, 8.5)[w], round_xn(2, i, misc[1])),
                      ((8, 10.5)[w], copy(k_tok.rearrange("p t d -> p (t d)"), misc[0][:], k_ready, i + 1, k_copied,
                                (k_link, 2 * i))),
                      ((11.5, 12.5)[w], values_T(i)), ((12.5, 12.5)[w], values_tok(i)), ((12.5, 13)[w], first_tap(i)),
                      ((13.5, 13.5)[w], copy(ogate[:], misc[1][:], og_ready, i + 1, og_done, (oT_done, i)))]
                if n is not None:
                    at += [((1.5, 4.5)[w], round_xn(1, n, misc[1])), ((7.5, 9)[w], sigmoids(1, n)), ((15, 16.5)[w], copy_wT(1, n, misc[1]))]
                run_phase(place(*at), work, before[-1:], silu, round_h, 1)

            def cut_weights(e):
                def piece():
                    n = (e + 1) // 2
                    act.wait_ge(w_loaded[n], 64 if n else 48)
                    nc.scalar.activation(w_hi[:, e], uncut(e)[:, 0], ACT.Copy).then_inc(w_hi_done, 1)
                return piece

            act.wait_ge(router_loaded, 16)
            nc.scalar.activation(router_cut[:, 0], router_raw, ACT.Copy).then_inc(router_hi_done, 1)
            cut_weights(0)()
            round_xn(1, 0, misc[1])()
            cut_weights(1)()
            cut_weights(2)()
            sigmoids(1, 0)()
            cut_weights(3)()
            cut_weights(4)()
            run_phase(place((0, cut_weights(5)), (0, cut_weights(6)), (0.5, copy_wT(1, 0, misc[1])),
                            (0, cut_weights(7)), (1, cut_weights(8)),
                            (4.5, round_xn(1, 1, misc[1])), (8.5, sigmoids(1, 1)),
                            (9.5, copy(aw_hi[:], aw_raw, attn_loaded, 80, attn_hi_done)),
                            (14.5, copy_wT(1, 1, misc[1]))), every(F1(0)), [], silu, round_h, 1)
            act.wait_ge(w_lo_pool_done, NE - BY_DVE)
            act.wait_ge(const_loaded, 160)
            phase_b(0, spaced(F1(1), 0, WIDE[0]), last(F1(0)), None)
            phase_a(1, spaced(F1(1), FIRST, WIDE[1]), last(F1(1), FIRST), None)
            with act.Fori(1, B - 1) as i:
                phase_b(i, every(F2(i - 1)), last(F1(i)), i + 1)
                phase_a(i + 1, every(F1(i + 1)), last(F2(i - 1)), i - 1)
            phase_b(B - 1, spaced(F2(B - 2), 0, WIDE[0]), last(F1(B - 1)), None)
            phase_a(B, spaced(F2(B - 2), FIRST, WIDE[1]), last(F2(B - 2), FIRST), None)
            run_phase(place((2.5, copy_out(F2(B - 2), 3))), every(F2(B - 1)), last(F2(B - 2))[-1:], silu, round_h, 1)
            for step in last(F2(B - 1))[-1:]:
                round_h(*step)
            copy_out(F2(B - 1), 3)()

        @block.gpsimd
        def _(pool):
            def weigh(p, k):
                l, c, before = p
                n, e = count(p, k), k // HALVES - 1
                if e < 0:
                    return
                if k % HALVES == 0 and e % (E // WD) == 0:
                    pool.wait_ge(w_bc_loaded[l][e * WD // E], 16 * c + 16)
                pool.wait_ge(silu_done, n)
                wait(pool, h_done, n - 3)
                nc.gpsimd.tensor_tensor(gw[:, k % 3, :], g[:, k % 3, :], w_bc[side(l, c)][:, e, :],
                                        ALU.mult).then_inc(gw_done, 1)

            def add_q(c):
                def piece():
                    pool.wait_ge(q_cos_done, c + 1)
                    pool.wait_ge(q_sin_done, c + 1)
                    wait(pool, num_ready, c)
                    nc.gpsimd.tensor_tensor(q_rot[:], qc[:], qs[:], ALU.add).then_inc(q_rot_done, 1)
                return piece

            def turn_k(c):
                half = DK // 2

                def heads(ap, a, b):
                    return ap.rearrange("p t (h d) -> p t h d", h=NH)[:, :, :, a:b]

                def table(ap, a, b):
                    return ap[:].rearrange("p t (o d) -> p t o d", o=1)[:, :, :, a:b].to_broadcast([P, T, NH, b - a])

                def cos_part():
                    pool.wait_ge(k_copied, c + 1)
                    wait(pool, kv_ready, c)
                    nc.gpsimd.tensor_tensor(heads(k_rot[:], 0, DK), heads(k_tok, 0, DK), table(cost, 0, DK), ALU.mult)

                def sin_part():
                    nc.gpsimd.tensor_tensor(heads(ks_, 0, half), heads(k_tok, half, DK), table(sint, 0, half),
                                            ALU.mult).then_inc(k_link, 1)
                    nc.gpsimd.tensor_tensor(heads(ks_, half, DK), heads(k_tok, 0, half), table(sint, half, DK),
                                            ALU.mult).then_inc(k_link, 1)

                def add_parts():
                    pool.wait_ge(k_link, 2 * c + 2)
                    nc.gpsimd.tensor_tensor(k_rot[:], k_rot[:], ks_, ALU.add).then_inc(k_rot_done, 1)
                return cos_part, sin_part, add_parts

            def phase_a(i, work):
                run_phase({}, work, [], weigh, None, 0)

            def phase_b(i, work):
                w = None in work
                k = turn_k(i)
                run_phase(place(((7.5, 10.5)[w], k[0]), ((10, 11)[w], k[1]), ((10, 13)[w], k[2]), ((12.5, 12.5)[w], add_q(i))),
                          work, [], weigh, None, 0)

            nc.gpsimd.memset(vT[:], 0.0)
            nc.gpsimd.memset(v_tok[:], 1.0).then_inc(pads_set, 1)
            for e in range(BY_DVE, NE):
                pool.wait_ge(w_hi_done, e + 1)
                nc.gpsimd.tensor_tensor(w_lo[:, e], uncut(e)[:, 0], w_hi[:, e].bitcast(F32),
                                        ALU.subtract).then_inc(w_lo_pool_done, 1)
            run_phase({}, every(F1(0)), [], weigh, None, 0)
            phase_b(0, spaced(F1(1), 0, WIDE[0]))
            phase_a(1, spaced(F1(1), FIRST, WIDE[1]))
            with pool.Fori(1, B - 1) as i:
                phase_b(i, every(F2(i - 1)))
                phase_a(i + 1, every(F1(i + 1)))
            phase_b(B - 1, spaced(F2(B - 2), 0, WIDE[0]))
            phase_a(B, spaced(F2(B - 2), FIRST, WIDE[1]))
            run_phase({}, every(F2(B - 1)), [], weigh, None, 0)

        @block.vector
        def _(dve):
            v = nc.vector

            def chain(s, base):
                made = []

                def link(issue):
                    n = len(made)

                    def piece():
                        if n:
                            dve.wait_ge(s, base + n)
                        issue().then_inc(s, 1)
                    made.append(piece)
                    return piece
                link.made = made
                return link

            def hidden(p, k):
                n = count(p, k)
                dve.wait_ge(up_ready, n)
                if k < HALVES:
                    dve.wait_ge(silu_done, n)
                    src = g
                else:
                    dve.wait_ge(gw_done, p[2] * ROUTED + k - HALVES + 1)
                    src = gw
                wait(dve, hi_done, n - 2)
                wait(dve, lo_done, n - 2)
                v.tensor_tensor(h[:, k % 2, :], src[:, k % 3, :], up_ps[k % 3][:], ALU.mult).then_inc(h_done, 1)

            def cut_h(p, k):
                n = count(p, k)
                dve.wait_ge(hi_done, n)
                v.tensor_tensor(h_lo[:, k % HR, :], h[:, k % 2, :], h_hi[:, k % HR, :].bitcast(F32),
                                ALU.subtract).then_inc(lo_done, 1)

            def ln(l, c, src, ready, value):
                link = chain(ln_link[l], c * LN_LINKS)

                def partial():
                    dve.wait_ge(ready, value)
                    for t in range(T):
                        ins = v.bn_stats(stats[:, t, :], src[:, t, :])
                    return ins

                def aggregate():
                    v.memset(nt[:], 0.0)
                    for t in range(T):
                        ins = v.bn_aggr(mv[:, t, :], stats[:, t, :])
                    return ins

                def exponent():
                    v.tensor_scalar(vh[:], ve[:], -0.5, None, ALU.mult)
                    return v.tensor_scalar(nt[:].bitcast(I32), ve[:].bitcast(I32), 1, None,
                                           ALU.logical_shift_right)

                moments = (link(partial), link(aggregate),
                           link(lambda: v.tensor_scalar(ve[:], mv[:, :, 1], EPS, None, ALU.add)))
                root = (link(exponent),
                        link(lambda: v.tensor_scalar(rstd[:].bitcast(I32), nt[:].bitcast(I32), -1.0,
                                                     float(RSQRT_MAGIC), ALU.mult, ALU.add)))
                newton = ()
                for _ in range(NEWTON):
                    newton += (link(lambda: v.tensor_tensor(nt[:], rstd[:], rstd[:], ALU.mult)),
                               link(lambda: v.tensor_tensor(nt[:], nt[:], vh[:], ALU.mult)),
                               link(lambda: v.scalar_tensor_tensor(out=rstd[:], in0=nt[:], scalar=1.5, in1=rstd[:],
                                                                   op0=ALU.add, op1=ALU.mult)))
                assert len(link.made) == LN_LINKS

                def normalize():
                    dve.wait_ge(ln_link[l], (c + 1) * LN_LINKS)
                    wait(dve, xnT_ready[l], c)
                    for t in range(T):
                        ins = v.tensor_scalar(xn[l][:, t, :], src[:, t, :], mv[:, t, 0:1], rstd[:, t:t + 1],
                                              ALU.subtract, ALU.mult)
                    ins.then_inc(xn_done[l], 1)
                return moments, root + newton, (normalize,)

            def cut_xn(l, c, bank):
                def piece():
                    dve.wait_ge(xt_hi_done[l], c + 1)
                    m_hi, m_lo = xt_hi[side(l, c)], xt_lo[side(l, c)]
                    v.tensor_tensor(m_lo[:], bank[:], m_hi[:].bitcast(F32),
                                    ALU.subtract).then_inc(xt_lo_done[l], 1)
                return piece

            def route(l, c, bank):
                link = chain(route_link[l], c * ROUTE_LINKS)
                L, neg, pos, pt = lg[l], lneg[l], lpos[l], rt[l]
                mine = pr[l][:].rearrange("p t (e o) -> p t e o", o=1).to_broadcast([P, T, E, E])
                others = pr[l][:].rearrange("p t (o j) -> p t o j", o=1).to_broadcast([P, T, E, E])
                lower = tri_sb[:].rearrange("p (o e) j -> p o e j", o=1).to_broadcast([P, T, E, E])

                halves = bank[:, 0:2 * T * E].rearrange("p (t r e) -> p t r e", t=T, r=2)

                def biased():
                    dve.wait_ge(logits_ready[l], c + 1)
                    return v.tensor_tensor(L[:], halves[:, :, 0],
                                           rbias_sb[:].rearrange("p (o e) -> p o e", o=1).to_broadcast([P, T, E]),
                                           ALU.add)

                def clamp():
                    dve.wait_ge(route_link[l], c * ROUTE_LINKS + 2)
                    v.tensor_scalar(neg[:], L[:], -1.0, None, ALU.min)
                    v.tensor_scalar(pos[:], L[:], -1.0, None, ALU.max).then_inc(clamped[l], 1)

                def inverse():
                    dve.wait_ge(clamped[l], c + 1)
                    return v.reciprocal(pt[:, 2], neg[:])

                def branches():
                    dve.wait_ge(sig_done[l], c + 1)
                    v.tensor_tensor(pt[:, 0], pt[:, 0], pt[:, 2], ALU.mult)
                    return v.tensor_scalar(pt[:, 1], pt[:, 1], 0.5, 0.5, ALU.mult, ALU.add)

                def chosen():
                    v.scalar_tensor_tensor(out=pt[:, 0], in0=L[:], scalar=-1.0, in1=pt[:, 0],
                                           op0=ALU.is_lt, op1=ALU.mult)
                    return v.scalar_tensor_tensor(out=pt[:, 1], in0=L[:], scalar=-1.0, in1=pt[:, 1],
                                                  op0=ALU.is_ge, op1=ALU.mult)

                def compare():
                    v.tensor_tensor(beats[:], others, mine, ALU.is_gt)
                    return v.tensor_tensor(ties[:], others, mine, ALU.is_equal)

                first = (link(biased), link(lambda: v.tensor_tensor(L[:], L[:], halves[:, :, 1], ALU.add)), clamp)
                probs = (link(inverse), link(branches), link(chosen),
                         link(lambda: v.tensor_tensor(pr[l][:], pt[:, 0], pt[:, 1], ALU.add)))
                ranks = (link(compare),
                         link(lambda: v.tensor_tensor(ties[:], ties[:], lower, ALU.mult)),
                         link(lambda: v.tensor_tensor(beats[:], beats[:], ties[:], ALU.add)),
                         link(lambda: v.tensor_reduce(rank[:], beats[:], AX.X, ALU.add)))
                top2 = (link(lambda: v.scalar_tensor_tensor(out=pr[l][:], in0=rank[:], scalar=1.5, in1=pr[l][:],
                                                            op0=ALU.is_lt, op1=ALU.mult)),
                        link(lambda: v.tensor_reduce(top[:], pr[l][:], AX.X, ALU.add)),
                        link(lambda: v.reciprocal(top[:], top[:])))
                assert len(link.made) == ROUTE_LINKS, len(link.made)

                def weights():
                    dve.wait_ge(route_link[l], (c + 1) * ROUTE_LINKS)
                    wait(dve, wT_ready[l], c)
                    v.tensor_tensor(wtok[l][:].rearrange("p e t -> p t e"), pr[l][:],
                                    top[:].rearrange("p (t o) -> p t o", o=1).to_broadcast([P, T, E]),
                                    ALU.mult).then_inc(wtok_done[l], 1)
                return first, probs, ranks, top2 + (weights,)

            def add_y(l, c, bank, dst, res, done, *waits):
                def piece():
                    dve.wait_ge(y_tok_ready[l], c + 1)
                    for s, n in waits:
                        wait(dve, s, n)
                    v.scalar_tensor_tensor(out=dst[:].rearrange("p t d -> p (t d)"), in0=bank[:], scalar=0.5,
                                           in1=res[:].rearrange("p t d -> p (t d)"),
                                           op0=ALU.mult, op1=ALU.add).then_inc(done, 1)
                return piece

            def q_part(c, bank, table, dst, ready, done):
                def piece():
                    dve.wait_ge(ready, c + 1)
                    wait(dve, q_rot_done, c)
                    v.tensor_tensor(dst[:], bank[:], table[:], ALU.mult).then_inc(done, 1)
                return piece

            def add_tap(c, j):
                def piece():
                    if j == 1:
                        dve.wait_ge(conv0_done, c + 1)
                    else:
                        dve.wait_ge(conv_link, (TAPS - 1) * c + j - 1)
                    v.scalar_tensor_tensor(out=conv, in0=vT[:, j:j + S], scalar=taps[:, j:j + 1], in1=conv,
                                           op0=ALU.mult, op1=ALU.add).then_inc(conv_link, 1)
                return piece

            def mask_kv(c, bank):
                def piece():
                    dve.wait_ge(kv_ready, c + 1)
                    wait(dve, num_ready, c)
                    v.tensor_tensor(kv_bd[:], bank[:, 0:D], bmask[:], ALU.mult)
                    v.tensor_scalar(ks_bd[:], hmask[:], bank[:, D:D + 1], None, ALU.mult).then_inc(kv_bd_done, 1)
                return piece

            def invert(c, bank):
                def piece():
                    dve.wait_ge(den_ready, c + 1)
                    v.tensor_scalar(den[:], bank[:, 0:T * NH], float(S), None, ALU.add).then_inc(den_link, 1)
                    dve.wait_ge(den_link, c + 1)
                    wait(dve, rdenT_ready, c)
                    v.reciprocal(rden[:], den[:]).then_inc(rden_done, 1)
                return piece

            def attend(c, bank):
                def piece():
                    dve.wait_ge(num_ready, c + 1)
                    dve.wait_ge(rbc_done, c + 1)
                    dve.wait_ge(vT_done, c + 1)
                    wait(dve, oT_done, c)
                    v.scalar_tensor_tensor(out=att, in0=bank[:], scalar=vsum[:, 0:1], in1=rden_bc[:],
                                           op0=ALU.add, op1=ALU.mult).then_inc(att_done, 1)
                return piece

            def apply_gate(c):
                def piece():
                    dve.wait_ge(att_done, c + 1)
                    dve.wait_ge(conv_link, 4 * c + 4)
                    v.tensor_tensor(att, att, conv, ALU.add).then_inc(o_sum_done, 1)
                    dve.wait_ge(o_sum_done, c + 1)
                    dve.wait_ge(og_done, c + 1)
                    wait(dve, proj_ready, c)
                    v.tensor_tensor(oT, att, ogate[:], ALU.mult).then_inc(oT_done, 1)
                return piece

            def x2_of(c):
                return x2 if side(3, c) == 3 else x_ln

            def add_attention(c, bank):
                def piece():
                    dve.wait_ge(proj_ready, c + 1)
                    if side(3, c) == 3:
                        wait(dve, x3_done, c)
                    v.tensor_tensor(x2_of(c)[:].rearrange("p t d -> p (t d)"), bank[:],
                                    x1[:].rearrange("p t d -> p (t d)"), ALU.add).then_inc(x2_done, 1)
                return piece

            def phase_a(i, work, before, o, nxt):
                w = None in work
                c = i - 1
                (m, n, norm), r = ln(3, c, x2_of(c), x2_done, c + 1), route(3, c, misc[0])
                at = [((1.5, 0.5)[w], add_tap(c, 4)), ((0, 0)[w], invert(c, misc[1])), ((4, 3)[w], attend(c, misc[0])), ((5, 3.5)[w], apply_gate(c)),
                      ((6, 4)[w], add_attention(c, misc[0])),
                      ((6, 6)[w], m[0]), ((6, 6)[w], m[1:]), ((6, 6.5)[w], n[0:2]), ((6.5, 6.5)[w], n[2:5]),
                      ((8, 7)[w], n[5:8]), ((8.5, 7.5)[w], n[8:]), ((8.5, 7.5)[w], norm),
                      ((10, 10.5)[w], cut_xn(3, c, misc[1])), ((11.5, 12)[w], r[0]), ((11.5, 13)[w], r[1][0:2]), ((11.5, 13)[w], r[1][2:]),
                      ((12, 13)[w], r[2][0:2]), ((12.5, 13)[w], r[2][2:]), ((14.5, 13.5)[w], r[3])]
                if o is not None:
                    at.append(((5.5, 6.5)[w], add_y(3, o, misc[1], x3, x2, x3_done, (x3_free, 16 * o + 16))))
                if nxt is not None:
                    m, n, norm = ln(1, nxt, x_ln, x_ln_loaded, 16 * nxt + 16)
                    at += [((0.5, 0)[w], m[0]),
                           ((1, 0)[w], m[1:]),
                           ((1, 0)[w], n[0:2]),
                           ((1.5, 0.5)[w], n[2:5]),
                           ((2, 1)[w], n[5:8]),
                           ((4, 2.5)[w], n[8:]),
                           ((5.5, 3)[w], norm)]
                run_steps(place(*at), work, before)

            def phase_b(i, work, before, nxt):
                w = None in work
                m, n, norm = ln(2, i, x1, x1_done, i + 1)
                at = []
                if nxt is not None:
                    at += [((2.5, 5.5)[w], cut_xn(1, nxt, misc[1]))]
                at += [((5, 4)[w], add_y(1, i, misc[1], x1, x_res, x1_done, (x_res_loaded, 16 * i + 16), (x2_done, i))),
                      ((5.5, 4.5)[w], m[0]), ((5.5, 5)[w], m[1:]), ((6, 5)[w], n[0:2]), ((6.5, 5.5)[w], n[2:5]),
                      ((6.5, 6.5)[w], n[5:8]), ((6.5, 6.5)[w], n[8:]), ((7, 7)[w], norm),
                      ((7.5, 9.5)[w], cut_xn(2, i, misc[1])), ((11, 11.5)[w], q_part(i, misc[0], cosf, qc, q_ready, q_cos_done)),
                      ((11, 12.5)[w], q_part(i, misc[1], sinf, qs, qp_ready, q_sin_done)), ((15.5, 17)[w], mask_kv(i, misc[0])),
                      ((14.5, 14)[w], add_tap(i, 1)), ((15, 16)[w], add_tap(i, 2)), ((16.5, 17.5)[w], add_tap(i, 3))]
                if nxt is not None:
                    r = route(1, nxt, misc[0])
                    at += [((4.5, 8.5)[w], r[0]), ((9.5, 10.5)[w], r[1][0:2]), ((10.5, 11)[w], r[1][2:]),
                      ((12, 12)[w], r[2][0:2]), ((13.5, 12.5)[w], r[2][2:]), ((14.5, 13)[w], r[3])]
                run_steps(place(*at), work, before)

            def run_steps(at, work, before):
                order = before + [step for step in work if step]
                n = len(before)
                for k in range(STEPS):
                    if work[k] and n >= 1:
                        hidden(*order[n - 1])
                    for piece in at.get(k, ()):
                        piece()
                    if work[k] and n >= 2:
                        cut_h(*order[n - 2])
                    for piece in at.get(k + 0.5, ()):
                        piece()
                    n += 1 if work[k] else 0

            def cut_weights(e):
                def piece():
                    dve.wait_ge(w_hi_done, e + 1)
                    v.tensor_tensor(w_lo[:, e], uncut(e)[:, 0], w_hi[:, e].bitcast(F32), ALU.subtract).then_inc(w_lo_done, 1)
                return piece

            def cut_attn():
                dve.wait_ge(attn_hi_done, 1)
                v.tensor_tensor(aw_lo[:], aw_raw, aw_hi[:].bitcast(F32),
                                ALU.subtract).then_inc(attn_lo_done, 1)

            for part in ln(1, 0, x_ln, x_ln_loaded, 16):
                for piece in part:
                    piece()
            dve.wait_ge(router_hi_done, 1)
            v.tensor_tensor(router_cut[:, 1], router_raw, router_cut[:, 0].bitcast(F32), ALU.subtract).then_inc(router_lo_done, 1)
            cut_xn(1, 0, misc[1])()
            cut_weights(0)()
            cut_weights(1)()
            cut_weights(2)()
            dve.wait_ge(ident_loaded, 48)
            first_route = route(1, 0, misc[0])
            for piece in first_route[0]:
                piece()
            for part in first_route[1:]:
                for piece in part:
                    piece()
            (m, n, norm), r = ln(1, 1, x_ln, x_ln_loaded, 32), route(1, 1, misc[0])
            run_steps(place((0, cut_weights(3)), (1, m[0]), (1.5, m[1:]), (2.5, n[0:2]), (2.5, n[2:5]),
                      (2.5, n[5:8]), (2.5, n[8:]), (2.5, norm),
                            (5.5, cut_xn(1, 1, misc[1])), (7, r[0]), (8.5, r[1][0:2]), (9, r[1][2:]),
                      (9.5, r[2][0:2]), (10.5, r[2][2:]), (10.5, r[3]),
                            (14.5, cut_attn)), every(F1(0)), [])
            dve.wait_ge(const_loaded, 160)
            dve.wait_ge(pads_set, 1)
            phase_b(0, spaced(F1(1), 0, WIDE[0]), last(F1(0))[-2:], None)
            phase_a(1, spaced(F1(1), FIRST, WIDE[1]), last(F1(1), FIRST)[-2:], None, 2)

            def middle(i, nxt):
                phase_b(i, every(F2(i - 1)), last(F1(i))[-2:], i + 1)
                phase_a(i + 1, every(F1(i + 1)), last(F2(i - 1))[-2:], i - 1, nxt)
            with dve.Fori(1, B - 2) as i:
                middle(i, i + 2)
            middle(B - 2, None)
            phase_b(B - 1, spaced(F2(B - 2), 0, WIDE[0]), last(F1(B - 1))[-2:], None)
            phase_a(B, spaced(F2(B - 2), FIRST, WIDE[1]), last(F2(B - 2), FIRST)[-2:], None, None)
            run_steps(place((6.5, add_y(3, B - 2, misc[1], x3, x2, x3_done, (x3_free, 16 * B - 16)))), every(F2(B - 1)),
                      last(F2(B - 2))[-2:])
            hidden(F2(B - 1), STEPS - 1)
            cut_h(F2(B - 1), STEPS - 2)
            cut_h(F2(B - 1), STEPS - 1)
            add_y(3, B - 1, misc[1], x3, x_ln, x3_done, (x3_free, 16 * B))()

    return nc


def shape_constants():
    f = np.float32
    inv = (f(1.0) / f(10000.0) ** (np.arange(0, DK, 2, dtype=f) / f(DK))).astype(f)
    freq = np.arange(S, dtype=f)[:, None] * inv[None, :]
    emb = np.concatenate([freq, freq], axis=-1)
    cos, sin = np.cos(emb).astype(f), np.sin(emb).astype(f)
    sin[:, :DK // 2] *= f(-1.0)
    head = np.arange(D) // DK
    scale = f(DK ** -0.5)
    expand = np.zeros((T * NH, T, D), f)
    for t in range(T):
        for hd in range(NH):
            expand[t * NH + hd, t, head == hd] = 1.0
    return {
        "cos_f": np.ascontiguousarray(np.tile(cos, (1, NH)).T), "sin_f": np.ascontiguousarray(np.tile(sin, (1, NH)).T),
        "cos_t": cos, "sin_t": sin,
        "blockmask": (head[:, None] == head[None, :]).astype(f) * scale,
        "headmask": (head[:, None] == np.arange(NH)[None, :]).astype(f) * scale,
        "expand": expand,
        "tri": (np.arange(E)[None, :] < np.arange(E)[:, None]).astype(f).reshape(1, E * E),
        "ident_in": np.eye(P, dtype=f),
    }


def kernel(**inputs):
    import concourse.bacc as bacc
    from concourse.bass_utils import run_bass_kernel_spmd

    a = {n: np.asarray(v) for n, v in inputs.items()}
    wqT = a["L0_attn_Wq"].T
    arrays = {
        "x": a["L0_attn_hidden_states"],
        "wq": wqT, "wqp": wqT.reshape(D, NH, 2, DK // 2)[:, :, ::-1, :].reshape(D, D),
        "wk": a["L0_attn_Wk"].T, "wv": a["L0_attn_Wv"].T, "wg": a["L0_attn_Wg"].T, "wo": a["L0_attn_Wo"].T,
        "lepe_w": a["L0_attn_lepe_w"], "lepe_b": a["L0_attn_lepe_b"],
        "sgate": a["L0_ffn_shared_gate"].T, "sup": a["L0_ffn_shared_up"].T, "sdown": a["L0_ffn_shared_down"].T,
        "gate_w": a["L0_ffn_gate_w"], "up_w": a["L0_ffn_up_w"], "down_w": a["L0_ffn_down_w"],
        "router": a["L0_ffn_router_w"].T, "rbias": a["L0_ffn_routing_bias"],
    }
    arrays.update(shape_constants())
    nc = bacc.Bacc("TRN2", target_bir_lowering=False, num_devices=1)
    named, args = {}, {}
    for name, array in arrays.items():
        named[f"{name}_dram"] = np.ascontiguousarray(array)
        args[name] = nc.dram_tensor(f"{name}_dram", array.shape, F32, kind="ExternalInput").ap()
    args["out"] = nc.dram_tensor("out_dram", [B, S, D], F32, kind="ExternalOutput").ap()
    build(nc, **args)
    r = run_bass_kernel_spmd(nc, [named], core_ids=[0])
    return r.results[0]["out_dram"]
```
